# Optimizing a Trainium2 kernel written in Bass

```python
import numpy as np
import jax
import jax.numpy as jnp

def _softmax(x, axis=-1):
    return jax.nn.softmax(x, axis=axis)

def _gelu(x):
    return jax.nn.gelu(x, approximate=True)

def _silu(x):
    return jax.nn.silu(x)

def _sigmoid(x):
    return jax.nn.sigmoid(x)

def _layernorm(x, axis=-1, eps=1e-05):
    m = jnp.mean(x, axis=axis, keepdims=True)
    v = jnp.var(x, axis=axis, keepdims=True)
    return (x - m) / jnp.sqrt(v + eps)

def _scatter_add(tgt, idx, src, axis=0):
    return tgt.at[idx].add(src)

def _segment_sum(src, seg, n):
    return jax.ops.segment_sum(src, seg, n)
kernel_name = 'mk_adaln_d1_jaxref_r4_48d38d'

def setup_inputs(seed: int=0):
    np.random.seed(seed)
    _w = jnp.asarray

    def _L0_attn_setup():
        import jax, jax.numpy as jnp
        import numpy as np
        B, S, D_IN = (4, 512, 256)
        EMBED, HEADS = (256, 16)
        HEAD_DIM = EMBED // HEADS
        key = jax.random.key(seed)
        k1, k2, k3 = jax.random.split(key, 3)
        x = jax.random.normal(k1, (B, S, D_IN), dtype=jnp.float32)
        lim_qkv = float(np.sqrt(6.0 / (D_IN + 3 * EMBED)))
        lim_o = float(np.sqrt(6.0 / (EMBED + EMBED)))
        w_qkv = jax.random.uniform(k2, (3 * EMBED, D_IN), minval=-lim_qkv, maxval=lim_qkv, dtype=jnp.float32)
        b_qkv = jnp.zeros((3 * EMBED,), dtype=jnp.float32)
        w_o = jax.random.uniform(k3, (EMBED, EMBED), minval=-lim_o, maxval=lim_o, dtype=jnp.float32)
        b_o = jnp.zeros((EMBED,), dtype=jnp.float32)
        return {'x': x, 'w_qkv': w_qkv, 'b_qkv': b_qkv, 'w_o': w_o, 'b_o': b_o}
    _L0_attn_in = _L0_attn_setup()

    def _L0_ffn_setup():
        import jax, jax.numpy as jnp
        import numpy as np
        H = 256
        I = 128
        E = 32
        TOP_K = 6
        N_GROUP = 8
        TOPK_GROUP = 4
        SCALE = 2.5
        N_SHARED = 2
        SI = I * N_SHARED
        B, S = (2, 256)
        key = jax.random.key(seed)
        ks = jax.random.split(key, 8)
        x = jax.random.normal(ks[0], (B, S, H), jnp.float32)
        gate_weight = jax.random.normal(ks[1], (E, H), jnp.float32) * 0.02
        e_score_correction_bias = jax.random.normal(ks[2], (E,), jnp.float32) * 0.01
        experts_gate_up = jax.random.normal(ks[3], (E, 2 * I, H), jnp.float32) * 0.02
        experts_down = jax.random.normal(ks[4], (E, H, I), jnp.float32) * 0.02
        shared_gate_w = jax.random.normal(ks[5], (SI, H), jnp.float32) * 0.02
        shared_up_w = jax.random.normal(ks[6], (SI, H), jnp.float32) * 0.02
        shared_down_w = jax.random.normal(ks[7], (H, SI), jnp.float32) * 0.02
        return {'x': x, 'gate_weight': gate_weight, 'e_score_correction_bias': e_score_correction_bias, 'experts_gate_up': experts_gate_up, 'experts_down': experts_down, 'shared_gate_w': shared_gate_w, 'shared_up_w': shared_up_w, 'shared_down_w': shared_down_w}
    _L0_ffn_in = _L0_ffn_setup()
    _L0_c = _w((lambda *s: np.random.randn(*s).astype(np.float32) * 0.05)(4, 256))
    _L0_wmod = _w((lambda *s: np.random.randn(*s).astype(np.float32) * 0.05)(256, 6 * 256) * 256 ** (-0.5))
    _d = {'L0_attn_x': _L0_attn_in['x'], 'L0_attn_w_qkv': _L0_attn_in['w_qkv'], 'L0_attn_b_qkv': _L0_attn_in['b_qkv'], 'L0_attn_w_o': _L0_attn_in['w_o'], 'L0_attn_b_o': _L0_attn_in['b_o'], 'L0_ffn_gate_weight': _L0_ffn_in['gate_weight'], 'L0_ffn_e_score_correction_bias': _L0_ffn_in['e_score_correction_bias'], 'L0_ffn_experts_gate_up': _L0_ffn_in['experts_gate_up'], 'L0_ffn_experts_down': _L0_ffn_in['experts_down'], 'L0_ffn_shared_gate_w': _L0_ffn_in['shared_gate_w'], 'L0_ffn_shared_up_w': _L0_ffn_in['shared_up_w'], 'L0_ffn_shared_down_w': _L0_ffn_in['shared_down_w'], 'L0_c': _L0_c, 'L0_wmod': _L0_wmod}
    _x0 = _d['L0_attn_x']
    _d['L0_attn_x'] = jax.random.normal(jax.random.fold_in(jax.random.key(seed), 1), (4, 1024, 256), dtype=_x0.dtype)
    del _x0
    return _d

def reference(L0_attn_x, L0_attn_w_qkv, L0_attn_b_qkv, L0_attn_w_o, L0_attn_b_o, L0_ffn_gate_weight, L0_ffn_e_score_correction_bias, L0_ffn_experts_gate_up, L0_ffn_experts_down, L0_ffn_shared_gate_w, L0_ffn_shared_up_w, L0_ffn_shared_down_w, L0_c, L0_wmod):

    def _L0_attn_ref(x, w_qkv, b_qkv, w_o, b_o):
        import jax, jax.numpy as jnp
        import numpy as np
        B, S, D_IN = (4, 512, 256)
        EMBED, HEADS = (256, 16)
        HEAD_DIM = EMBED // HEADS
        b, s, _ = x.shape
        qkv = jnp.einsum('bsi,oi->bso', x, w_qkv) + b_qkv
        qkv = qkv.reshape(b, s, HEADS, 3 * HEAD_DIM).transpose(0, 2, 1, 3)
        q, k, v = jnp.split(qkv, 3, axis=-1)
        scale = 1.0 / jnp.sqrt(jnp.float32(HEAD_DIM))
        attn = jnp.einsum('bhqd,bhkd->bhqk', q, k) * scale
        attn = jax.nn.softmax(attn, axis=-1)
        vals = jnp.einsum('bhqk,bhkd->bhqd', attn, v)
        vals = vals.reshape(b, s, EMBED)
        out = jnp.einsum('bse,oe->bso', vals, w_o) + b_o
        return out

    def _L0_ffn_ref(x, gate_weight, e_score_correction_bias, experts_gate_up, experts_down, shared_gate_w, shared_up_w, shared_down_w):
        import jax, jax.numpy as jnp
        import numpy as np
        H = 256
        I = 128
        E = 32
        TOP_K = 6
        N_GROUP = 8
        TOPK_GROUP = 4
        SCALE = 2.5
        N_SHARED = 2
        SI = I * N_SHARED
        B, S = (2, 256)
        b, s, h = x.shape
        xf = x.reshape(-1, h)
        T = xf.shape[0]
        logits = xf.astype(jnp.float32) @ gate_weight.astype(jnp.float32).T
        scores = jax.nn.sigmoid(logits)
        sfc = scores + e_score_correction_bias[None, :]
        gs = E // N_GROUP
        group_scores = sfc.reshape(T, N_GROUP, gs).max(axis=-1)
        _, gidx = jax.lax.top_k(group_scores, TOPK_GROUP)
        gmask = jnp.zeros((T, N_GROUP), bool).at[jnp.arange(T)[:, None], gidx].set(True)
        smask = jnp.repeat(gmask, gs, axis=1)
        masked = jnp.where(smask, sfc, 0.0)
        _, topk_idx = jax.lax.top_k(masked, TOP_K)
        tw = jnp.take_along_axis(scores, topk_idx, axis=1)
        tw = tw / (tw.sum(-1, keepdims=True) + 1e-20)
        tw = (tw * SCALE).astype(xf.dtype)
        combine = jnp.zeros((T, E), xf.dtype).at[jnp.arange(T)[:, None], topk_idx].add(tw)

        def expert_step(acc, inp):
            gu, dn, c = inp
            g = xf @ gu[:I].T
            u = xf @ gu[I:].T
            o = jax.nn.silu(g) * u @ dn.T
            return (acc + c[:, None] * o, None)
        routed, _ = jax.lax.scan(expert_step, jnp.zeros_like(xf), (experts_gate_up, experts_down, combine.T))
        sh = jax.nn.silu(xf @ shared_gate_w.T) * (xf @ shared_up_w.T)
        shared_out = sh @ shared_down_w.T
        return (routed + shared_out).reshape(b, s, h)
    x = L0_attn_x
    mod = (_silu(L0_c) @ L0_wmod).reshape(L0_c.shape[0], 6, 1, -1)
    sa, ca, ga, sb, cb, gb = (mod[:, 0], mod[:, 1], mod[:, 2], mod[:, 3], mod[:, 4], mod[:, 5])
    ga = (2 * (ga >= 0) - 1) * jnp.maximum(jnp.abs(ga), 0.25)
    gb = (2 * (gb >= 0) - 1) * jnp.maximum(jnp.abs(gb), 0.25)
    h = _layernorm(x, axis=-1) * (1 + ca) + sa
    x = x + ga * _L0_attn_ref(h, L0_attn_w_qkv, L0_attn_b_qkv, L0_attn_w_o, L0_attn_b_o)
    h = _layernorm(x, axis=-1) * (1 + cb) + sb
    x = x + gb * _L0_ffn_ref(h, L0_ffn_gate_weight, L0_ffn_e_score_correction_bias, L0_ffn_experts_gate_up, L0_ffn_experts_down, L0_ffn_shared_gate_w, L0_ffn_shared_up_w, L0_ffn_shared_down_w)
    return x

_drawn_inputs = setup_inputs


def setup_inputs(seed=0):
    import zlib

    import numpy as np

    out = dict(_drawn_inputs(seed))
    spreads = {'L0_attn_b_qkv': (0.0, 0.312), 'L0_attn_b_o': (0.0, 0.314)}
    factors = {'L0_attn_w_qkv': 4.29,
     'L0_ffn_gate_weight': 8.0,
     'L0_ffn_e_score_correction_bias': 8.0,
     'L0_ffn_experts_gate_up': 8.0,
     'L0_ffn_experts_down': 8.0,
     'L0_ffn_shared_gate_w': 8.0,
     'L0_ffn_shared_up_w': 8.0,
     'L0_ffn_shared_down_w': 8.0}
    for name, (base, spread) in spreads.items():
        noise = np.random.default_rng([zlib.crc32(name.encode()), seed]).standard_normal(out[name].shape)
        drawn = base * np.exp(spread * noise) if base else spread * noise
        out[name] = jnp.asarray(drawn.astype(out[name].dtype))
    for name, factor in factors.items():
        out[name] = (out[name] * factor).astype(out[name].dtype)
    return out
```

```python
from contextlib import ExitStack

import concourse.bass as bass
from concourse import mybir
from concourse.alu_op_type import AluOpType as ALU

ACT = mybir.ActivationFunctionType
F32 = mybir.dt.float32
BF16 = mybir.dt.bfloat16
I32 = mybir.dt.int32
AX = mybir.AxisListType

P = 128
B, S, D = 4, 1024, 256
H, HD = 16, 16
T = B * S
KC = D // P
CH = 512
TPC = CH // P
CPB = S // CH
LN_EPS = 1e-5
HG = 4
NG = H // HG
KT = S // P
QROWS = 6 * HD
Q_PART = (0, 0, 0, 1, 1, 2)
K_PART = (0, 1, 2, 0, 1, 0)
HI, MID, LO = range(3)
E, TOPK = 32, 6
GROUPS, TOPG = 8, 4
EPG = E // GROUPS
INTER = 128
SHARED = 256
ROUTED_SCALE = 2.5
TILES = (T * TOPK - E) // P + E
CAP = T + P
LIST_ROWS = E * CAP + E * P
ROW = D + E
RES_ROWS = T * TOPK + 2 * E * P
SA, CA, GA, SB_, CB, GB = range(6)


class Env:
    pass


def wait(eng, sem, value):
    if not isinstance(value, int) or value > 0:
        eng.wait_ge(sem, value)


class Chain:

    def __init__(self, eng, sem, base=0):
        self.eng, self.sem, self.count, self.links = eng, sem, base, 0

    def link(self, instruction):
        instruction.then_inc(self.sem, 1)
        self.count = self.count + 1
        self.links += 1
        self.eng.wait_ge(self.sem, self.count)

    def loop(self, first, end, links, body):
        start = self.count
        with self.eng.Fori(first, end) as i:
            self.count, self.links = start + (i - first) * links, 0
            body(i)
            assert self.links == links, self.links
        self.count = start + (end - first) * links


def mean_and_variance(nc, chain, mean, var, diff, stats, varied):
    even, odd = stats[:, :, 1], stats[:, :, 4]
    nc.vector.tensor_tensor(mean, even, odd, ALU.add)
    nc.vector.tensor_tensor(diff, even, odd, ALU.subtract)
    chain.link(nc.vector.tensor_tensor(var, stats[:, :, 2], stats[:, :, 5], ALU.add))
    nc.vector.tensor_scalar(mean, mean, 0.5, None, ALU.mult)
    nc.vector.tensor_scalar(var, var, 1.0 / D, LN_EPS, ALU.mult, ALU.add)
    chain.link(nc.vector.tensor_tensor(diff, diff, diff, ALU.mult))
    nc.vector.scalar_tensor_tensor(out=var, in0=diff, scalar=0.25, in1=var, op0=ALU.mult,
                                   op1=ALU.add).then_inc(varied, 1)


def inverse_deviation(nc, chain, out, scratch, std, var):
    chain.link(nc.vector.reciprocal(out, std))
    chain.link(nc.vector.tensor_tensor(scratch, out, out, ALU.mult))
    chain.link(nc.vector.tensor_tensor(scratch, scratch, var, ALU.mult))
    chain.link(nc.vector.tensor_scalar(scratch, scratch, -0.5, 1.5, ALU.mult, ALU.add))
    chain.link(nc.vector.tensor_tensor(out, out, scratch, ALU.mult))


def setup_phase(nc, env):
    with ExitStack() as ctx:
        def sb(name, shape, dt):
            return ctx.enter_context(nc.sbuf_tensor(name, shape, dt))

        cT = sb("cT", [P, KC, B], F32)
        scT = sb("scT", [P, KC, B], F32)
        sc_rep = sb("sc_rep", [P, KC, B, P], F32)
        wmod_sb = sb("wmod_sb", [P, KC, 6 * D], F32)
        sign = sb("sign", [P, 2, B, D], F32)
        mag = sb("mag", [P, 2, B, D], F32)
        psC = ctx.enter_context(nc.psum_tensor("psC", [P, 4, KC, B], F32))
        psB = ctx.enter_context(nc.psum_tensor("psB", [P, 4, 512], F32))
        loads, silu, rep, chan, bcast, copied, ch, zero = (env.sem(n) for n in (
            "setup_loads", "setup_silu", "setup_rep", "setup_chan", "setup_bcast", "setup_copied", "setup_chain",
            "setup_zero"))
        n_loads = 5
        block = ctx.enter_context(nc.Block())

        @block.sync
        def _(sp):
            sp.dma_start(cT[:], env.cT.rearrange("(k p) b -> p k b", p=P)).then_inc(loads, 16)
            sp.dma_start(wmod_sb[:], env.wmod.rearrange("(k p) n -> p k n", p=P)).then_inc(loads, 16)
            sp.dma_start(env.wqkv[:], env.wqkvT.rearrange("s (k p) n -> p s k n", p=P)).then_inc(loads, 16)
            sp.dma_start(env.bqk[:], env.bqk_d).then_inc(loads, 16)
            sp.dma_start(env.bv_bc[:], env.bv_d.to_broadcast([P, D])).then_inc(loads, 16)
            sp.wait_ge(loads, 16 * n_loads)

        @block.gpsimd
        def _(pool):
            nc.gpsimd.memset(env.ident[:], 0.0).then_inc(zero, 1)
            pool.wait_ge(zero, 1)
            nc.gpsimd.affine_select(out=env.ident[:], in_=env.ident[:], compare_op=ALU.not_equal, fill=1.0, base=0,
                                    pattern=[[-1, P]], channel_multiplier=1).then_inc(zero, 1)
            pool.wait_ge(zero, 2)

        @block.scalar
        def _(act):
            act.wait_ge(loads, 16 * n_loads)
            nc.scalar.activation(scT[:], cT[:], ACT.Silu).then_inc(silu, 1)

        @block.vector
        def _(dve):
            c = Chain(dve, ch)
            dve.wait_ge(silu, 1)
            nc.vector.tensor_copy(sc_rep[:].rearrange("p k b r -> p (k b) r"),
                                  scT[:].rearrange("p k b -> p (k b)").unsqueeze(2).to_broadcast([P, KC * B, P])
                                  ).then_inc(rep, 1)
            dve.wait_ge(chan, 1)
            c.link(nc.vector.tensor_copy(env.modc[:, 0::2], psC[:, 0::2]))
            c.link(nc.vector.tensor_scalar(env.modc[:, 1::2], psC[:, 1::2], 1.0, None, ALU.add))
            for n in range(2 * B):
                b, half = n // 2, n % 2
                dve.wait_ge(bcast, n + 1)
                nc.vector.tensor_copy(env.modb[:, b, 2 * half:2 * half + 2].rearrange("p a d -> p (a d)"),
                                      psB[:, n % 4]).then_inc(copied, 1)
            dve.wait_ge(copied, 2 * B)
            for n, kind in enumerate((0, 3)):
                g = env.modb[:, :, kind]
                c.link(nc.vector.tensor_scalar(sign[:, n], g, 0.0, 2.0, ALU.is_ge, ALU.mult))
                c.link(nc.vector.tensor_scalar(mag[:, n], g, -1.0, None, ALU.mult))
                c.link(nc.vector.tensor_tensor(mag[:, n], mag[:, n], g, ALU.max))
                c.link(nc.vector.tensor_scalar(mag[:, n], mag[:, n], 0.25, None, ALU.max))
                c.link(nc.vector.tensor_scalar(sign[:, n], sign[:, n], -1.0, None, ALU.add))
                c.link(nc.vector.tensor_tensor(g, sign[:, n], mag[:, n], ALU.mult))
            c.link(nc.vector.tensor_scalar(env.modb[:, :, 2], env.modb[:, :, 2], 1.0, None, ALU.add))

        @block.tensor
        def _(pe):
            pe.wait_ge(silu, 1)
            for n, kind in enumerate((SA, CA, SB_, CB)):
                for m in range(KC):
                    for k in range(KC):
                        last = nc.tensor.matmul(psC[:, n, m], wmod_sb[:, k, kind * D + m * P:kind * D + m * P + P],
                                                scT[:, k], start=(k == 0), stop=(k == KC - 1))
            last.then_inc(chan, 1)
            pe.wait_ge(rep, 1)
            for n in range(2 * B):
                b, half = n // 2, n % 2
                if n >= 4:
                    pe.wait_ge(copied, n - 3)
                for k in range(KC):
                    mm = nc.tensor.matmul(psB[:, n % 4], sc_rep[:, k, b],
                                          wmod_sb[:, k, 2 * D + half * 512:2 * D + half * 512 + 512],
                                          start=(k == 0), stop=(k == KC - 1))
                mm.then_inc(bcast, 1)


def projection_phase(nc, env):
    NCH = B * CPB
    QKT = 2 * KC
    with ExitStack() as ctx:
        def sb(name, shape, dt):
            return ctx.enter_context(nc.sbuf_tensor(name, shape, dt))

        xin = sb("xin", [P, 2, TPC, D], F32)
        stats = sb("stats", [P, 2, TPC, 6], F32)
        mean = sb("mean", [P, 2, TPC], F32)
        diff = sb("diff", [P, 2, TPC], F32)
        std = sb("std", [P, 2, TPC], F32)
        rstd = sb("rstd", [P, 2, TPC], F32)
        var = sb("var", [P, 2, TPC], F32)
        newton = sb("newton", [P, 2, TPC], F32)
        xhat = sb("xhat", [P, 2, TPC, D], F32)
        hT = sb("hT", [P, 2, KC, CH], F32)
        full = sb("full", [P, QKT, CH], F32)
        rest = sb("rest", [P, QKT, CH], F32)
        parts = sb("parts", [P, QKT, 3, CH], BF16)
        vst = sb("vst", [P, 2, TPC, H, 2 * HD], F32)
        psT = ctx.enter_context(nc.psum_tensor("psT", [P, KC, CH], F32))
        psQK = ctx.enter_context(nc.psum_tensor("psQK", [P, QKT, CH], F32))
        psV = ctx.enter_context(nc.psum_tensor("psV", [P, 2, 2, D], F32))
        (varied, std_ok, normed, turned, modulated, qk_done, p0_ok, r_ok, p1_ok, p2_ok, v_done, v_ok, ones_ok,
         ch) = (env.sem("proj_" + n) for n in (
            "varied", "std_ok", "normed", "turned", "modulated", "qk_done", "p0_ok", "r_ok", "p1_ok",
            "p2_ok", "v_done", "v_ok", "ones_ok", "chain"))
        x_in, v_stored = ([env.sem(f"proj_{n}{u}") for u in range(CPB)] for n in ("x_in", "v_stored"))
        qk_stored = [env.sem(f"proj_qk_stored{j}") for j in range(QKT)]
        x_d = env.x.rearrange("(c i p) d -> c p i d", i=TPC, p=P)

        def over_batches(eng, body):
            body(0, False)
            with eng.Fori(1, B - 1) as b:
                body(b, False)
            body(B - 1, True)

        block = ctx.enter_context(nc.Block())

        @block.sync
        def _(sp):
            def load(c, u):
                wait(sp, normed, c - 1)
                sp.dma_start(xin[:, u], x_d[bass.ds(c, 1)].rearrange("o p i d -> (o p) i d")).then_inc(x_in[u], 16)

            def store(c, b, u):
                for j in range(QKT):
                    sp.wait_ge(p2_ok, QKT * c + j + 1)
                    sp.dma_start(env.qk_parts[j // KC, :, bass.ds(b, 1), j % KC, :, u * CH:(u + 1) * CH].rearrange(
                        "s o p t -> p (s o) t"), parts[:, j]).then_inc(qk_stored[j], 16)
                sp.wait_ge(v_ok, 2 * (c + 1))
                for g in range(NG):
                    sp.dma_start(env.v_d[bass.ds(b, 1), g, :, u * TPC:(u + 1) * TPC].rearrange("o p k n -> (o p) k n"),
                                 vst[:, u, :, g * HG:(g + 1) * HG, :].rearrange("p i h n -> p i (h n)")
                                 ).then_inc(v_stored[u], 16)

            def body(b, last):
                for u in range(CPB):
                    c = b * CPB + u
                    if not last:
                        load(c + 2, u)
                    store(c, b, u)

            load(0, 0)
            load(1, 1)
            over_batches(sp, body)
            for j in range(QKT):
                sp.wait_ge(qk_stored[j], 16 * NCH)
            for u in range(CPB):
                sp.wait_ge(v_stored[u], 16 * NG * B)

        @block.vector
        def _(dve):
            LN_LINKS = 8

            def norm(c, b, u):
                chain = Chain(dve, ch, LN_LINKS * c)
                dve.wait_ge(x_in[u], 16 * (b + 1))
                for i in range(TPC):
                    ins = nc.vector.bn_stats(stats[:, u, i], xin[:, u, i])
                chain.link(ins)
                mean_and_variance(nc, chain, mean[:, u], var[:, u], diff[:, u], stats[:, u], varied)
                dve.wait_ge(std_ok, c + 1)
                inverse_deviation(nc, chain, rstd[:, u], newton[:, u], std[:, u], var[:, u])
                wait(dve, turned, KC * (c - 1))
                for i in range(TPC):
                    ins = nc.vector.tensor_scalar(xhat[:, u, i], xin[:, u, i], mean[:, u, i:i + 1], rstd[:, u, i:i + 1],
                                                  ALU.subtract, ALU.mult)
                ins.then_inc(normed, 1)

            def split(c, j):
                dve.wait_ge(p0_ok, QKT * c + j + 1)
                nc.vector.tensor_tensor(rest[:, j], full[:, j], parts[:, j, HI], ALU.subtract).then_inc(r_ok, 1)

            def split_last(c, j):
                dve.wait_ge(p1_ok, QKT * c + j + 1)
                nc.vector.tensor_tensor(parts[:, j, LO], rest[:, j], parts[:, j, MID], ALU.subtract).then_inc(p2_ok, 1)

            def values(c, b, u):
                for n in range(2):
                    dve.wait_ge(v_done, 2 * c + n + 1)
                    if n == 0:
                        wait(dve, v_stored[u], 16 * NG * b)
                    nc.vector.tensor_tensor(
                        vst[:, u, 2 * n:2 * n + 2, :, 0:HD], psV[:, n].rearrange("p i (h d) -> p i h d", h=H),
                        env.bv_bc[:].rearrange("p (h d) -> p h d", h=H).unsqueeze(1).to_broadcast([P, 2, H, HD]),
                        ALU.add).then_inc(v_ok, 1)

            def body(b, last):
                for u in range(CPB):
                    c = b * CPB + u
                    if not (last and u == CPB - 1):
                        norm(c + 1, b + (u + 1) // 2, (u + 1) % 2)
                    for j in range(QKT):
                        split(c, j)
                        if j:
                            split_last(c, j - 1)
                    split_last(c, QKT - 1)
                    values(c, b, u)

            nc.vector.memset(vst[:, :, :, :, HD:2 * HD], 1.0).then_inc(ones_ok, 1)
            dve.wait_ge(ones_ok, 1)
            norm(0, 0, 0)
            over_batches(dve, body)

        @block.scalar
        def _(act):
            def deviation(c, u):
                act.wait_ge(varied, c + 1)
                nc.scalar.activation(std[:, u], var[:, u], ACT.Sqrt).then_inc(std_ok, 1)

            def modulate(c, b, u):
                for k in range(KC):
                    act.wait_ge(turned, KC * c + k + 1)
                    if k == 0:
                        wait(act, v_done, 2 * (c - 1))
                    nc.scalar.activation(hT[:, u, k], psT[:, k], ACT.Identity, bias=env.modc[:, 0, k, bass.ds(b, 1)],
                                         scale=env.modc[:, 1, k, bass.ds(b, 1)]).then_inc(modulated, 1)

            def evacuate(c, j):
                act.wait_ge(qk_done, QKT * c + j + 1)
                wait(act, qk_stored[j], 16 * c)
                bias = env.bqk[:, j // KC, j % KC:j % KC + 1]
                nc.scalar.activation(full[:, j], psQK[:, j], ACT.Identity, bias=bias)
                nc.scalar.activation(parts[:, j, HI], psQK[:, j], ACT.Identity, bias=bias).then_inc(p0_ok, 1)

            def second(c, j):
                act.wait_ge(r_ok, QKT * c + j + 1)
                nc.scalar.activation(parts[:, j, MID], rest[:, j], ACT.Copy).then_inc(p1_ok, 1)

            def body(b, last):
                for u in range(CPB):
                    c = b * CPB + u
                    if not (last and u == CPB - 1):
                        deviation(c + 1, (u + 1) % 2)
                    for j in range(QKT):
                        evacuate(c, j)
                        if j:
                            second(c, j - 1)
                    second(c, QKT - 1)
                    if not (last and u == CPB - 1):
                        modulate(c + 1, b + (u + 1) // 2, (u + 1) % 2)

            deviation(0, 0)
            modulate(0, 0, 0)
            over_batches(act, body)

        @block.tensor
        def _(pe):
            def turn(c, u):
                pe.wait_ge(normed, c + 1)
                wait(pe, modulated, KC * c)
                for k in range(KC):
                    for i in range(TPC):
                        mm = nc.tensor.transpose(psT[:, k, i * P:(i + 1) * P], xhat[:, u, i, k * P:(k + 1) * P],
                                                 env.ident[:])
                    mm.then_inc(turned, 1)

            def queries_keys(c, u):
                pe.wait_ge(modulated, KC * (c + 1))
                for j in range(QKT):
                    wait(pe, p0_ok, QKT * (c - 1) + j + 1)
                    for k in range(KC):
                        mm = nc.tensor.matmul(psQK[:, j], env.wqkv[:, j // KC, k, (j % KC) * P:(j % KC) * P + P],
                                              hT[:, u, k], start=(k == 0), stop=(k == KC - 1))
                    mm.then_inc(qk_done, 1)

            def values(c, u):
                for n in range(2):
                    wait(pe, v_ok, 2 * (c - 1) + n + 1)
                    for i in range(2):
                        for k in range(KC):
                            mm = nc.tensor.matmul(psV[:, n, i], hT[:, u, k, (2 * n + i) * P:(2 * n + i + 1) * P],
                                                  env.wqkv[:, 2, k, :], start=(k == 0), stop=(k == KC - 1))
                    mm.then_inc(v_done, 1)

            def body(b, last):
                for u in range(CPB):
                    c = b * CPB + u
                    queries_keys(c, u)
                    if not (last and u == CPB - 1):
                        turn(c + 1, (u + 1) % 2)
                    values(c, u)

            turn(0, 0)
            over_batches(pe, body)


def attention_phase(nc, env):
    QH = S // 512
    STEPS = QH * KT
    UNITS = HG * (S // P) * 2
    UNITS_AT_STEP = 5
    RING = 3
    LOADS = 13
    NGR = B * NG
    with ExitStack() as ctx:
        def sb(name, shape, dt):
            return ctx.enter_context(nc.sbuf_tensor(name, shape, dt))

        qa = [sb(f"q_rows{g}", [QROWS + 1, HG, S], BF16) for g in range(NG)]
        ka = [sb(f"k_rows{g}", [QROWS + 1, HG, S], BF16) for g in range(NG)]
        va = [sb(f"v_cols{g}", [P, KT, HG * 2 * HD], F32) for g in range(NG)]
        probs = sb("probs", [P, 2, HG, 512], F32)
        o_sb = sb("o_sb", [P, HD, S // HD], F32)
        piece_max = sb("piece_max", [P, 2, HG * KT], F32)
        row_max = sb("row_max", [P, HG * KT], F32)
        neg_max = sb("neg_max", [P, HG * KT], BF16)
        neg_max_t = sb("neg_max_t", [P, HG * KT], BF16)
        psE = ctx.enter_context(nc.psum_tensor("psE", [P, 2, 2, 512], F32))
        psM = ctx.enter_context(nc.psum_tensor("psM", [P, RING, 512], F32))
        psO = ctx.enter_context(nc.psum_tensor("psO", [P, 512], F32))
        (ones_ok, scored, exp_ok, summed, piece_done, piece_read, max_ready, max_stored, max_there, o_read, ch) = (
            env.sem("att_" + n) for n in ("ones_ok", "scored", "exp_ok", "summed", "piece_done", "piece_read",
                                          "max_ready", "max_stored", "max_there", "o_read", "chain"))
        loaded = [env.sem(f"att_loaded{g}") for g in range(NG)]
        o_stored = env.sem("att_o_stored")

        def over_batches(eng, body):
            body(0, False)
            with eng.Fori(1, B - 1) as b:
                body(b, False)
            body(B - 1, True)

        def units_of(s):
            return range(min(UNITS, UNITS_AT_STEP * s), min(UNITS, UNITS_AT_STEP * (s + 1)))

        block = ctx.enter_context(nc.Block())

        @block.sync
        def _(sp):
            def load(b, g):
                for r in range(6):
                    for n, (rows, part) in enumerate(((qa, Q_PART[r]), (ka, K_PART[r]))):
                        sp.dma_start(
                            rows[g][HD * r:HD * (r + 1)],
                            env.qk_parts[n, part, bass.ds(b, 1), g // 2, (g % 2) * HG * HD:(g % 2 + 1) * HG * HD, :]
                            .rearrange("o (h d) t -> (o d) h t", d=HD)).then_inc(loaded[g], 16)
                sp.dma_start(va[g][:], env.v_d[bass.ds(b, 1), g].rearrange("o p k n -> (o p) k n")
                             ).then_inc(loaded[g], 16)

            def put_max(group, g):
                sp.wait_ge(max_ready, group + 1)
                for n in range(P // 32):
                    sp.dma_start(env.max_d[:, n], neg_max_t[32 * n:32 * n + 32, :]).then_inc(max_stored, 16)
                sp.wait_ge(max_stored, 4 * 16 * (group + 1))
                sp.dma_start(qa[g][QROWS:QROWS + 1].rearrange("o h t -> o (h t)"),
                             env.max_d.rearrange("h n r -> (h n r)").unsqueeze(0)).then_inc(max_there, 16)

            def store(b, g):
                sp.wait_ge(o_read, QH * (b * NG + g + 1))
                sp.dma_start(env.o_d[bass.ds(b, 1), g].rearrange("o p r a -> (o p) r a"), o_sb[:]
                             ).then_inc(o_stored, 16)

            def body(b, last):
                for g in range(NG):
                    if not (last and g == NG - 1):
                        put_max(b * NG + g + 1, (g + 1) % NG)
                    if not last:
                        sp.wait_ge(summed, STEPS * (b * NG + g + 1))
                        load(b + 1, g)
                    store(b, g)

            for g in range(NG):
                load(0, g)
            put_max(0, 0)
            over_batches(sp, body)
            sp.wait_ge(o_stored, 16 * NGR)

        @block.vector
        def _(dve):
            LINKS = 2

            def piece_maximum(group, n):
                dve.wait_ge(piece_done, UNITS * group + n + 1)
                return nc.vector.tensor_reduce(piece_max[:, n % 2, n // 2:n // 2 + 1], psM[:, n % RING], AX.X,
                                               ALU.max).then_inc(piece_read, 1)

            def finish(group):
                chain = Chain(dve, ch, LINKS * group)
                dve.wait_ge(piece_read, UNITS * (group + 1))
                chain.link(nc.vector.tensor_tensor(row_max[:], piece_max[:, 0], piece_max[:, 1], ALU.max))
                chain.link(nc.vector.tensor_scalar(neg_max[:], row_max[:], -1.0, None, ALU.mult))
                wait(dve, max_stored, 4 * 16 * group)
                nc.vector.transpose(neg_max_t[:], neg_max[:]).then_inc(max_ready, 1)

            def body(b, last):
                for g in range(NG):
                    group = b * NG + g + 1
                    if last and g == NG - 1:
                        continue
                    for n in range(UNITS):
                        piece_maximum(group, n)
                    finish(group)

            for g in range(NG):
                nc.vector.memset(ka[g][QROWS:QROWS + 1], 1.0).then_inc(ones_ok, 1)
            for n in range(UNITS):
                piece_maximum(0, n)
            finish(0)
            over_batches(dve, body)

        @block.scalar
        def _(act):
            def copy_out(b, g, qh):
                act.wait_ge(summed, STEPS * (b * NG + g) + KT * (qh + 1))
                if qh == 0:
                    wait(act, o_stored, 16 * (b * NG + g))
                nc.scalar.activation(o_sb[:, :, qh * 32:(qh + 1) * 32], psO[:].rearrange("p (a r) -> p r a", r=HD),
                                     ACT.Copy).then_inc(o_read, 1)

            def body(b, last):
                for g in range(NG):
                    for s in range(STEPS):
                        step = STEPS * (b * NG + g) + s
                        for pair in range(2):
                            act.wait_ge(scored, 2 * step + pair + 1)
                            if pair == 0:
                                wait(act, summed, step - 1)
                            nc.scalar.activation(
                                probs[:, s % 2, 2 * pair:2 * pair + 2], psE[:, pair], ACT.Exp,
                                scale=HD ** -0.5).then_inc(exp_ok, 1)
                        if s == KT:
                            copy_out(b, g, 0)
                        if s == 0 and not (isinstance(b, int) and b == 0 and g == 0):
                            copy_out(b, g - 1, 1)

            over_batches(act, body)
            copy_out(B - 1, NG - 1, 1)

        @block.tensor
        def _(pe):
            def piece(group, g, n):
                qt, h, kh = (n // 2) % KT, n // (2 * KT), n % 2
                used = n - RING if n >= RING else (-1, -3, -2)[n]
                wait(pe, piece_read, UNITS * group + used + 1)
                nc.tensor.matmul(psM[:, n % RING], qa[g][0:QROWS, h, qt * P:(qt + 1) * P],
                                 ka[g][0:QROWS, h, kh * 512:(kh + 1) * 512], start=True, stop=True
                                 ).then_inc(piece_done, 1)

            def scores(step, g, s, pair):
                wait(pe, exp_ok, 2 * (step - 1) + pair + 1)
                qh, kt = s // KT, s % KT
                for i in range(2):
                    h = 2 * pair + i
                    mm = nc.tensor.matmul(psE[:, pair, i], ka[g][:, h, kt * P:(kt + 1) * P],
                                          qa[g][:, h, qh * 512:(qh + 1) * 512], start=True, stop=True)
                mm.then_inc(scored, 1)

            def weighted_values(group, g, s):
                qh, kt = s // KT, s % KT
                pe.wait_ge(exp_ok, 2 * (STEPS * group + s) + 2)
                if kt == 0:
                    wait(pe, o_read, QH * group + qh)
                for h in range(HG):
                    mm = nc.tensor.matmul(psO[32 * h:32 * h + 32], va[g][:, kt, 32 * h:32 * h + 32],
                                          probs[:, s % 2, h], start=(kt == 0), stop=(kt == KT - 1))
                mm.then_inc(summed, 1)

            def body(b, last):
                for g in range(NG):
                    group = b * NG + g
                    ahead = not (last and g == NG - 1)
                    pe.wait_ge(max_there, 16 * (group + 1))
                    if ahead:
                        pe.wait_ge(loaded[(g + 1) % NG], 16 * LOADS * (b + 1 + (g + 1) // NG))
                    for s in range(STEPS):
                        step = STEPS * group + s
                        units = list(units_of(s)) if ahead else []
                        scores(step, g, s, 0)
                        for n in units[:2]:
                            piece(group + 1, (g + 1) % NG, n)
                        scores(step, g, s, 1)
                        for n in units[2:]:
                            piece(group + 1, (g + 1) % NG, n)
                        if s:
                            weighted_values(group, g, s - 1)
                        elif not (isinstance(b, int) and b == 0 and g == 0):
                            weighted_values(group - 1, (g - 1) % NG, STEPS - 1)

            pe.wait_ge(ones_ok, NG)
            pe.wait_ge(loaded[0], 16 * LOADS)
            for n in range(UNITS):
                piece(0, 0, n)
            over_batches(pe, body)
            weighted_values(NGR - 1, NG - 1, STEPS - 1)


def route_phase(nc, env):
    NCH = B * CPB
    with ExitStack() as ctx:
        def sb(name, shape, dt=F32):
            return ctx.enter_context(nc.sbuf_tensor(name, shape, dt))

        def ps(name, shape, dt=F32):
            return ctx.enter_context(nc.psum_tensor(name, shape, dt))

        wo, wsd, wo_g, wsd_g = (sb(n, [P, KC, D]) for n in ("wo", "wsd", "wo_g", "wsd_g"))
        bo_bc, bo_g = (sb(n, [P, D]) for n in ("bo_bc", "bo_g"))
        gate_w = sb("gate_w", [P, KC, E])
        ebias = sb("ebias", [P, E])
        wsg = sb("wsg", [P, KC, 2 * SHARED])
        den, rden = (sb(n, [P, B, P]) for n in ("den", "rden"))
        num, rdn, vals, h2T = (sb(n, [P, 2, KC, CH]) for n in ("num", "rdn", "vals", "h2T"))
        xin, h2 = (sb(n, [P, 2, TPC, D]) for n in ("xin2", "h2"))
        xhat = sb("xhat2", [P, TPC, D])
        stats = sb("stats2", [P, TPC, 6])
        mean, diff, var, std, rstd, newton, wsum, wrec, tok6 = (sb(n, [P, TPC]) for n in (
            "mean2", "diff2", "var2", "std2", "rstd2", "newton2", "wsum", "wrec", "tok6"))
        rows = sb("rows", [P, 2, TPC, ROW])
        sc = sb("sc", [P, 2, TPC, E])
        sfc, masked, slot, dest = (sb(n, [P, TPC, E]) for n in ("sfc", "masked", "slot", "dest"))
        gmax, gmask, top, top_f = (sb(n, [P, TPC, 8]) for n in ("gmax", "gmask", "top", "top_f"))
        top_at = sb("top_at", [P, TPC, 8], mybir.dt.uint32)
        gmatch = sb("gmatch", [P, TPC, GROUPS, TOPG])
        hot, picked = (sb(n, [P, TPC, TOPK, E]) for n in ("hot", "picked"))
        sel = sb("sel", [P, TPC, E], BF16)
        w6 = sb("w6", [P, TPC, TOPK])
        count = sb("count", [P, TPC + 1, E])
        slot6 = sb("slot6", [P, 2, TPC, TOPK], I32)
        iota_e, list_at, pad_at, need_f, need_cum, ones_e = (sb(n, [P, E]) for n in (
            "iota_e", "list_at", "pad_at", "need_f", "need_cum", "ones_e"))
        pad_slot, need_i = (sb(n, [P, E], I32) for n in ("pad_slot", "need_i"))
        before, ones = (sb(n, [P, P], BF16) for n in ("before", "ones"))
        pad_row = sb("pad_row", [P, ROW])
        mark = sb("mark", [P, 1])
        spare_to = sb("spare_to", [P, E, E], I32)
        past, past_n = (sb(n, [P, 2, E]) for n in ("past", "past_n"))
        tile_no, tile_e, tile_c, tile_r = (sb(n, [P, 2]) for n in ("tile_no", "tile_e", "tile_c", "tile_r"))
        table = sb("table", [P, 2, 2], I32)
        silu, act_s = (sb(n, [P, 2, SHARED]) for n in ("silu", "act_s"))
        actT = sb("actT", [P, KC, P])

        psX = ps("psX", [P, TPC, D])
        psT = ps("psT2", [P, KC, CH])
        psG, psP, psS = (ps(n, [P, 512]) for n in ("psG", "psP", "psS"))
        psGU = ps("psGU", [P, 2 * SHARED])
        logits = psG[:, 0:TPC * E]
        (varied, std_ok, vals_ok, projected, x2_ok, h2_ok, rows_ok, turned, h2T_ok, gated, sc_ok, sel_ok, placed, routed,
         gu_done, silu_ok, a_ok, at_done, at_ok, y_done, y_read, wo_ok, wsd_ok, consts, const_in, den_in, rden_ok,
         rden_out, ch, spare_in, pads_ok, pads_out, table_ok, table_out, zeroed, marked) = (env.sem("rt_" + n) for n in (
            "varied", "std_ok", "vals_ok", "projected", "x2_ok", "h2_ok", "rows_ok", "turned", "h2T_ok", "gated",
            "sc_ok", "sel_ok", "placed", "routed", "gu_done", "silu_ok", "a_ok", "at_done", "at_ok", "y_done", "y_read",
            "wo_ok", "wsd_ok", "consts", "const_in", "den_in", "rden_ok", "rden_out", "chain", "spare_in", "pads_ok",
            "pads_out", "table_ok", "table_out", "zeroed", "marked"))
        ins, scattered = ([env.sem(f"rt_{n}{u}") for u in range(CPB)] for n in ("in", "scattered"))
        x_d = env.x.rearrange("(c i p) d -> c p i d", i=TPC, p=P)
        LOADS = 2 * HD + 1
        CONST_LOADS = 6
        CONSTS = 10

        def over_batches(eng, body):
            body(0, False)
            with eng.Fori(1, B - 1) as b:
                body(b, False)
            body(B - 1, True)

        def none_before(c):
            return isinstance(c, int) and c == 0

        block = ctx.enter_context(nc.Block())

        @block.sync
        def _(sp):
            for b in range(B):
                for a in range(S // P):
                    sp.dma_start(den[H * a:H * a + H, b], env.o_d[b].rearrange(
                        "g (j n) r a -> (g j) n (r a)", n=2 * HD)[:, HD, a * P:(a + 1) * P]).then_inc(den_in, 16)
            for to, of in ((wo, env.woT), (gate_w, env.gateT), (wsg, env.wsgT), (wsd, env.wsdT)):
                sp.dma_start(to[:], of.rearrange("(k p) n -> p k n", p=P)).then_inc(const_in, 16)
            sp.dma_start(bo_bc[:], env.bo_d.to_broadcast([P, D])).then_inc(const_in, 16)
            sp.dma_start(ebias[:], env.ebias_d.to_broadcast([P, E])).then_inc(const_in, 16)
            sp.wait_ge(rden_ok, 1)
            for b in range(B):
                for a in range(S // P):
                    sp.dma_start(env.rden_d[b, :, a * P:(a + 1) * P], rden[H * a:H * a + H, b]).then_inc(rden_out, 16)
            sp.wait_ge(rden_out, 16 * B * (S // P))

            def load(c, b, u):
                wait(sp, x2_ok, c - 1)
                sums = env.o_d[bass.ds(b, 1)].rearrange("o g (j n) r a -> (o g j) n r a", n=2 * HD)
                inverse = env.rden_d[bass.ds(b, 1)].rearrange("o h (r a) -> (o h) r a", r=HD)
                heads = slice(u * H // CPB, (u + 1) * H // CPB)
                for r in range(HD):
                    part = slice(HD * (r % 8), HD * (r % 8 + 1))
                    sp.dma_start(num[part, u, r // 8].rearrange("d (h a) -> d h a", h=H // CPB),
                                 sums[heads, 0:HD, r].rearrange("h d a -> d h a")).then_inc(ins[u], 16)
                    sp.dma_start(rdn[part, u, r // 8].rearrange("d (h a) -> d h a", h=H // CPB),
                                 inverse[heads, r].unsqueeze(0).to_broadcast([HD, H // CPB, S // HD])
                                 ).then_inc(ins[u], 16)
                sp.dma_start(xin[:, u], x_d[bass.ds(c, 1)].rearrange("o p i d -> (o p) i d")).then_inc(ins[u], 16)

            def body(b, last):
                for u in range(CPB):
                    load(b * CPB + u, b, u)

            over_batches(sp, body)
            sp.wait_ge(consts, CONSTS)
            spare = env.lists[E * CAP:LIST_ROWS].rearrange("(k p) n -> p k n", p=P)
            for k in range(E):
                sp.dma_start(spare[:, k, 0:D], pad_row[:, 0:D]).then_inc(spare_in, 16)
            sp.dma_start(spare[:, :, D:ROW], spare_to[:].bitcast(F32)).then_inc(spare_in, 16)
            sp.wait_ge(spare_in, 16 * (E + 1))
            sp.wait_ge(table_ok, 1)
            for n in range(2):
                sp.dma_start(env.table_d[n * P:(n + 1) * P], table[:, n]).then_inc(table_out, 16)
            sp.wait_ge(table_out, 32)

        @block.gpsimd
        def _(pool):
            g = nc.gpsimd
            floats = {"allow_small_or_imprecise_dtypes": True}
            g.memset(ones[:], 1.0).then_inc(consts, 1)
            g.iota(iota_e[:], [[1, E]], base=0, channel_multiplier=0, **floats).then_inc(consts, 1)
            g.iota(list_at[:], [[CAP, E]], base=0, channel_multiplier=0, **floats).then_inc(consts, 1)
            g.iota(pad_at[:], [[CAP, E]], base=0, channel_multiplier=1, **floats).then_inc(consts, 1)
            g.iota(tok6[:], [[TOPK * P, TPC]], base=0, channel_multiplier=TOPK, **floats).then_inc(consts, 1)
            g.iota(tile_no[:], [[P, 2]], base=0, channel_multiplier=1, **floats).then_inc(consts, 1)
            g.memset(pad_row[:, 0:D], 0.0).then_inc(consts, 1)
            g.iota(pad_row[:, D:ROW].bitcast(I32), [[P, E]], base=T * TOPK, channel_multiplier=1).then_inc(consts, 1)
            g.iota(spare_to[:], [[P, E], [0, E]], base=T * TOPK + E * P, channel_multiplier=1).then_inc(consts, 1)
            pool.wait_ge(consts, CONSTS - 1)
            g.affine_select(out=before[:], in_=ones[:], compare_op=ALU.is_gt, fill=0.0, base=0, pattern=[[1, P]],
                            channel_multiplier=-1).then_inc(consts, 1)

            def body(b, last):
                for u in range(CPB):
                    c = b * CPB + u
                    pool.wait_ge(rows_ok, c + 1)
                    pool.wait_ge(routed, c + 1)
                    wait(pool, marked, c)
                    g.tensor_tensor(mark[:], pad_row[:, 0:1], pad_row[:, 0:1], ALU.add).then_inc(marked, 1)
                    for i in range(TPC):
                        for j in range(TOPK):
                            g.indirect_dma_start(
                                env.lists[:, :], bass.IndirectOffsetOnAxis(ap=slot6[:, u, i, j:j + 1], axis=0),
                                rows[:, u, i, :], None).then_inc(scattered[u], 16)

            over_batches(pool, body)
            pool.wait_ge(pads_ok, 1)
            for e in range(E):
                g.indirect_dma_start(env.lists[:, :], bass.IndirectOffsetOnAxis(ap=pad_slot[:, e:e + 1], axis=0),
                                     pad_row[:, :], None).then_inc(pads_out, 16)
            for u in range(CPB):
                pool.wait_ge(scattered[u], 16 * B * TPC * TOPK)
            pool.wait_ge(pads_out, 16 * E)

        @block.scalar
        def _(act):
            a = nc.scalar

            def front(c, b, u):
                act.wait_ge(varied, c + 1)
                a.activation(std[:], var[:], ACT.Sqrt).then_inc(std_ok, 1)
                act.wait_ge(h2_ok, c + 1)
                wait(act, scattered[u], 16 * TPC * TOPK * b)
                a.activation(rows[:, u, :, 0:D], h2[:, u], ACT.Copy).then_inc(rows_ok, 1)
                for k in range(KC):
                    act.wait_ge(turned, KC * c + k + 1)
                    if k == 0:
                        wait(act, gu_done, TPC * (c - 1))
                    a.activation(h2T[:, u, k], psT[:, k], ACT.Copy).then_inc(h2T_ok, 1)
                act.wait_ge(gated, c + 1)
                wait(act, routed, c - 1)
                a.activation(sc[:, u].rearrange("p i e -> p (i e)"), logits, ACT.Sigmoid).then_inc(sc_ok, 1)

            def shared(c):
                for i in range(TPC):
                    t = TPC * c + i
                    act.wait_ge(gu_done, t + 1)
                    wait(act, a_ok, t - 1)
                    a.activation(silu[:, i % 2], psGU[:, 0:SHARED], ACT.Silu).then_inc(silu_ok, 1)
                    act.wait_ge(at_done, t + 1)
                    wait(act, y_done, t)
                    a.activation(actT[:].rearrange("p k t -> p (k t)"), psS[:, 0:SHARED], ACT.Copy).then_inc(at_ok, 1)

            def body(b, last):
                for u in range(CPB):
                    c = b * CPB + u
                    front(c, b, u)
                    if not none_before(c):
                        shared(c - 1)

            over_batches(act, body)
            shared(NCH - 1)

        @block.vector
        def _(dve):
            v = nc.vector
            chain = Chain(dve, ch)
            link = chain.link

            def bc(ap, *shape):
                return ap.to_broadcast([P, *shape])

            def scale_out(b):
                ga = env.modb[:, bass.ds(b, 1), 0, :]
                v.tensor_tensor(wo_g[:], wo[:], bc(ga, KC, D), ALU.mult)
                v.tensor_tensor(bo_g[:].unsqueeze(1), bo_bc[:].unsqueeze(1), ga, ALU.mult).then_inc(wo_ok, 1)
                dve.wait_ge(wo_ok, b + 1)

            def scale_shared(b):
                v.tensor_tensor(wsd_g[:], wsd[:], bc(env.modb[:, bass.ds(b, 1), 3, :], KC, D),
                                ALU.mult).then_inc(wsd_ok, 1)

            def values(c, b, u):
                dve.wait_ge(ins[u], 16 * LOADS * (b + 1))
                wait(dve, projected, c - 1)
                v.tensor_tensor(vals[:, u], num[:, u], rdn[:, u], ALU.mult).then_inc(vals_ok, 1)

            def front(c, b, u):
                def tile(i):
                    return env.x2[:, bass.ds(TPC * c + i, 1)].rearrange("p o d -> p (o d)")

                link(v.tensor_tensor(xin[:, u], xin[:, u], bc(bo_g[:].unsqueeze(1), TPC, D), ALU.add))
                dve.wait_ge(projected, c + 1)
                v.tensor_tensor(env.x2[:, bass.ds(TPC * c, TPC)], psX[:], xin[:, u], ALU.add).then_inc(x2_ok, 1)
                dve.wait_ge(x2_ok, c + 1)
                v.tensor_copy(mean[:, 0:1], bo_bc[:, 0:1])
                for i in range(TPC):
                    ins_ = v.bn_stats(stats[:, i], tile(i))
                link(ins_)
                mean_and_variance(nc, chain, mean[:], var[:], diff[:], stats[:], varied)
                dve.wait_ge(std_ok, c + 1)
                inverse_deviation(nc, chain, rstd[:], newton[:], std[:], var[:])
                for i in range(TPC):
                    ins_ = v.tensor_scalar(xhat[:, i], tile(i), mean[:, i:i + 1], rstd[:, i:i + 1], ALU.subtract,
                                           ALU.mult)
                link(ins_)
                link(v.tensor_tensor(xhat[:], xhat[:], bc(env.modb[:, bass.ds(b, 1), 2, :], TPC, D), ALU.mult))
                wait(dve, turned, KC * (c - 1))
                wait(dve, rows_ok, c - 1)
                v.tensor_tensor(h2[:, u], xhat[:], bc(env.modb[:, bass.ds(b, 1), 1, :], TPC, D),
                                ALU.add).then_inc(h2_ok, 1)
                dve.wait_ge(h2_ok, c + 1)

            def best(of):
                v.tensor_copy(top_f[:, :, 0:1], of[:, :, 0:1])
                for i in range(TPC):
                    ins_ = v.max(top[:, i], of[:, i])
                link(ins_)
                v.tensor_copy(top_f[:, :, 0:1], of[:, :, 0:1])
                for i in range(TPC):
                    ins_ = v.max_index(top_at[:, i], top[:, i], of[:, i])
                link(ins_)
                link(v.tensor_copy(top_f[:], top_at[:]))

            def pick(of, out):
                link(v.tensor_tensor(picked[:], hot[:], bc(of.unsqueeze(2), TPC, TOPK, E), ALU.mult))
                with nc.allow_low_precision(reason="whole numbers below 2 ** 24, or float32"):
                    link(v.tensor_reduce(out, picked[:], AX.X, ALU.add))

            def route(c, b, u):
                dve.wait_ge(sc_ok, c + 1)
                link(v.tensor_tensor(sfc[:], sc[:, u], bc(ebias[:].unsqueeze(1), TPC, E), ALU.add))
                link(v.tensor_reduce(gmax[:], sfc[:].rearrange("p i (g k) -> p i g k", g=GROUPS), AX.X, ALU.max))
                best(gmax)
                link(v.tensor_tensor(gmatch[:], bc(iota_e[:, 0:GROUPS].unsqueeze(1).unsqueeze(3), TPC, GROUPS, TOPG),
                                     bc(top_f[:, :, 0:TOPG].unsqueeze(2), TPC, GROUPS, TOPG), ALU.is_equal))
                link(v.tensor_reduce(gmask[:], gmatch[:], AX.X, ALU.max))
                for i in range(TPC):
                    ins_ = v.tensor_tensor(masked[:, i].rearrange("p (g k) -> p g k", g=GROUPS),
                                           sfc[:, i].rearrange("p (g k) -> p g k", g=GROUPS),
                                           bc(gmask[:, i].unsqueeze(2), GROUPS, EPG), ALU.mult)
                link(ins_)
                best(masked)
                link(v.tensor_tensor(hot[:], bc(iota_e[:].unsqueeze(1).unsqueeze(1), TPC, TOPK, E),
                                     bc(top_f[:, :, 0:TOPK].unsqueeze(3), TPC, TOPK, E), ALU.is_equal))
                with nc.allow_low_precision(reason="zeros and ones"):
                    v.tensor_reduce(sel[:], hot[:].rearrange("p i j e -> p i e j"), AX.X, ALU.max).then_inc(sel_ok, 1)
                pick(sc[:, u], w6[:])
                link(v.tensor_reduce(wsum[:], w6[:], AX.X, ALU.add))
                link(v.tensor_scalar(wsum[:], wsum[:], 1e-20, None, ALU.add))
                link(v.reciprocal(wrec[:], wsum[:]))
                v.scalar_tensor_tensor(out=env.weights[:, bass.ds(TPC * c, TPC)], in0=w6[:], scalar=ROUTED_SCALE,
                                       in1=bc(wrec[:].unsqueeze(2), TPC, TOPK), op0=ALU.mult, op1=ALU.mult)
                dve.wait_ge(placed, c + 1)
                for i in range(TPC):
                    link(v.tensor_tensor(count[:, i + 1], psP[:, (TPC + i) * E:(TPC + i + 1) * E], count[:, i],
                                         ALU.add))
                link(v.tensor_tensor(slot[:], psP[:, 0:TPC * E].rearrange("p (i e) -> p i e", i=TPC),
                                     count[:, 0:TPC], ALU.add))
                link(v.tensor_tensor(slot[:], slot[:], bc(list_at[:].unsqueeze(1), TPC, E), ALU.add))
                wait(dve, scattered[u], 16 * TPC * TOPK * b)
                pick(slot[:], slot6[:, u])
                link(v.tensor_tensor(picked[:], hot[:], bc(iota_e[:, 0:TOPK].unsqueeze(1).unsqueeze(3), TPC, TOPK, E),
                                     ALU.mult))
                link(v.tensor_reduce(dest[:], picked[:].rearrange("p i j e -> p i e j"), AX.X, ALU.max))
                v.tensor_tensor(rows[:, u, :, D:ROW].bitcast(I32), dest[:], bc(tok6[:].unsqueeze(2), TPC, E),
                                ALU.add).then_inc(routed, 1)
                dve.wait_ge(routed, c + 1)
                v.tensor_copy(count[:, 0], count[:, TPC])
                link(v.tensor_scalar(tok6[:], tok6[:], float(TOPK * CH), None, ALU.add))

            def shared(c):
                for i in range(TPC):
                    t = TPC * c + i
                    dve.wait_ge(silu_ok, t + 1)
                    v.tensor_tensor(act_s[:, i % 2], psGU[:, SHARED:], silu[:, i % 2], ALU.mult).then_inc(a_ok, 1)
                    dve.wait_ge(y_done, t + 1)
                    x2 = env.x2[:, bass.ds(t, 1)].rearrange("p o d -> p (o d)")
                    v.tensor_tensor(x2, psS[:, SHARED:], x2, ALU.add).then_inc(y_read, 1)

            dve.wait_ge(den_in, 16 * B * (S // P))
            v.reciprocal(rden[:], den[:]).then_inc(rden_ok, 1)
            v.memset(ones_e[:], 1.0).then_inc(zeroed, 1)
            v.memset(count[:, 0], 0.0).then_inc(zeroed, 1)
            dve.wait_ge(zeroed, 2)
            dve.wait_ge(const_in, 16 * CONST_LOADS)
            dve.wait_ge(consts, CONSTS)
            values(0, 0, 0)

            def body(b, last):
                for u in range(CPB):
                    c = b * CPB + u
                    if u == 0:
                        scale_out(b)
                    front(c, b, u)
                    if not (last and u == CPB - 1):
                        values(c + 1, b + u, (u + 1) % 2)
                    if not none_before(c):
                        route(c - 1, b - 1 + u, (u + 1) % 2)
                        shared(c - 1)
                    if u == 0:
                        scale_shared(b)

            body(0, False)
            chain.loop(1, B - 1, 78, lambda b: body(b, False))
            body(B - 1, True)
            route(NCH - 1, B - 1, CPB - 1)
            total = count[:, TPC]
            v.tensor_tensor(pad_slot[:], total, pad_at[:], ALU.add).then_inc(pads_ok, 1)
            link(v.tensor_scalar(need_i[:], total, float(P - 1), None, ALU.add))
            link(v.tensor_scalar(need_i[:], need_i[:], P.bit_length() - 1, None, ALU.arith_shift_right))
            link(v.tensor_copy(need_f[:], need_i[:]))
            link(v.tensor_tensor_scan(need_cum[:], ones_e[:], need_f[:], 0.0, ALU.mult, ALU.add))
            for n in range(2):
                ins_ = v.tensor_scalar(past[:, n], need_cum[:], tile_no[:, n:n + 1], None, ALU.is_le)
            link(ins_)
            v.tensor_reduce(tile_e[:], past[:], AX.X, ALU.add)
            link(v.tensor_tensor(past_n[:], past[:], bc(need_f[:].unsqueeze(1), 2, E), ALU.mult))
            link(v.tensor_reduce(tile_c[:], past_n[:], AX.X, ALU.add))
            link(v.tensor_tensor(tile_r[:], tile_no[:], tile_c[:], ALU.subtract))
            link(v.tensor_scalar(tile_c[:], tile_e[:], float(CAP), None, ALU.mult))
            v.scalar_tensor_tensor(out=table[:, :, 0], in0=tile_r[:], scalar=float(P), in1=tile_c[:], op0=ALU.mult,
                                   op1=ALU.add)
            v.tensor_scalar(table[:, :, 1], tile_e[:], float(E - 1), None, ALU.min).then_inc(table_ok, 1)
            shared(NCH - 1)

        @block.tensor
        def _(pe):
            t_ = nc.tensor

            def front(c, b, u):
                pe.wait_ge(vals_ok, c + 1)
                pe.wait_ge(wo_ok, b + 1)
                wait(pe, x2_ok, c)
                for i in range(TPC):
                    for m in range(KC):
                        mm = t_.matmul(psX[:, i], vals[:, u, m, i * P:(i + 1) * P], wo_g[:, m], start=(m == 0),
                                       stop=(m == KC - 1))
                mm.then_inc(projected, 1)
                pe.wait_ge(h2_ok, c + 1)
                wait(pe, h2T_ok, KC * c)
                for k in range(KC):
                    for i in range(TPC):
                        mm = t_.transpose(psT[:, k, i * P:(i + 1) * P], h2[:, u, i, k * P:(k + 1) * P], env.ident[:])
                    mm.then_inc(turned, 1)
                pe.wait_ge(h2T_ok, KC * (c + 1))
                wait(pe, sc_ok, c)
                for i in range(TPC):
                    for k in range(KC):
                        mm = t_.matmul(psG[:, i * E:(i + 1) * E], h2T[:, u, k, i * P:(i + 1) * P], gate_w[:, k],
                                       start=(k == 0), stop=(k == KC - 1))
                mm.then_inc(gated, 1)

            def place(c):
                pe.wait_ge(sel_ok, c + 1)
                wait(pe, routed, c)
                flat = sel[:].rearrange("p i e -> p (i e)")
                t_.matmul(psP[:, 0:TPC * E], before[:], flat, start=True, stop=True)
                t_.matmul(psP[:, TPC * E:2 * TPC * E], ones[:], flat, start=True, stop=True).then_inc(placed, 1)

            def shared(c, b, u):
                pe.wait_ge(wsd_ok, b + 1)
                for i in range(TPC):
                    t = TPC * c + i
                    wait(pe, a_ok, t)
                    for k in range(KC):
                        mm = t_.matmul(psGU[:], h2T[:, u, k, i * P:(i + 1) * P], wsg[:, k], start=(k == 0),
                                       stop=(k == KC - 1))
                    mm.then_inc(gu_done, 1)
                    pe.wait_ge(a_ok, t + 1)
                    wait(pe, y_read, t)
                    for m in range(KC):
                        mm = t_.transpose(psS[:, m * P:(m + 1) * P], act_s[:, i % 2, m * P:(m + 1) * P], env.ident[:])
                    mm.then_inc(at_done, 1)
                    pe.wait_ge(at_ok, t + 1)
                    for m in range(KC):
                        mm = t_.matmul(psS[:, SHARED:], actT[:, m], wsd_g[:, m], start=(m == 0), stop=(m == KC - 1))
                    mm.then_inc(y_done, 1)

            def body(b, last):
                for u in range(CPB):
                    c = b * CPB + u
                    front(c, b, u)
                    if not none_before(c):
                        place(c - 1)
                        shared(c - 1, b - 1 + u, (u + 1) % 2)

            over_batches(pe, body)
            place(NCH - 1)
            shared(NCH - 1, B - 1, CPB - 1)


def expert_phase(nc, env):
    DEEP = 4
    STEPS = TILES + 3
    with ExitStack() as ctx:
        def sb(name, shape, dt=F32):
            return ctx.enter_context(nc.sbuf_tensor(name, shape, dt))

        gu_w = sb("gu_w", [P, E, KC, 2 * INTER])
        down_w = sb("down_w", [P, E, D])
        place = sb("place", [1, 2 * P, 2], I32)
        rows = sb("ex_rows", [P, DEEP, ROW])
        xT = sb("ex_xT", [P, 2, D])
        silu, act_e, actT = (sb(n, [P, 2, INTER]) for n in ("ex_silu", "ex_act", "ex_actT"))
        y = sb("ex_y", [P, DEEP, D])
        dest = sb("ex_dest", [P, DEEP], I32)
        mark = sb("ex_mark", [P, 2])
        psX, psGU, psA, psY = (ctx.enter_context(nc.psum_tensor(n, [P, 2, 512], F32)) for n in (
            "ex_psX", "ex_psGU", "ex_psA", "ex_psY"))
        (weights_in, place_in, x_done, x_ok, dest_ok, gu_done, silu_ok, act_ok, a_done, a_ok, y_done, y_ok,
         marked) = (env.sem("ex_" + n) for n in (
            "weights_in", "place_in", "x_done", "x_ok", "dest_ok", "gu_done", "silu_ok", "act_ok", "a_done", "a_ok",
            "y_done", "y_ok", "marked"))
        rows_in, scattered = ([env.sem(f"ex_{n}{u}") for u in range(DEEP)] for n in ("rows_in", "scattered"))
        GROUP = 4
        WEIGHT_LOADS = 2 * E // GROUP

        def over_steps(eng, body):
            for s in range(2 * DEEP):
                body(s, s % DEEP)
            with eng.Fori(2, TILES // DEEP) as i:
                for u in range(DEEP):
                    body(DEEP * i + u, u)
            for s in range(TILES // DEEP * DEEP, STEPS):
                body(s, s % DEEP)

        def exists(t):
            return not isinstance(t, int) or 0 <= t < TILES

        def expert_of(eng, t):
            return eng.value_load(place[0:1, bass.ds(t, 1), 1], min_val=0, max_val=E - 1)

        block = ctx.enter_context(nc.Block())

        @block.sync
        def _(sp):
            sp.dma_start(place[:], env.table_d.unsqueeze(0)).then_inc(place_in, 16)
            for e in range(0, E, GROUP):
                sp.dma_start(gu_w[:, e:e + GROUP], env.guT[e:e + GROUP].rearrange("e (k p) n -> p e k n", p=P)
                             ).then_inc(weights_in, 16)
                sp.dma_start(down_w[:, e:e + GROUP], env.downT[e:e + GROUP].rearrange("e p n -> p e n")
                             ).then_inc(weights_in, 16)
            sp.wait_ge(place_in, 16)

            def body(t, u):
                if exists(t):
                    row = sp.value_load(place[0:1, bass.ds(t, 1), 0], min_val=0, max_val=LIST_ROWS - P)
                    wait(sp, x_done, t - DEEP + 1)
                    wait(sp, dest_ok, t - DEEP + 1)
                    sp.dma_start(rows[:, u], env.lists[bass.ds(row, P)]).then_inc(rows_in[u], 16)

            over_steps(sp, body)

        @block.tensor
        def _(pe):
            def body(t, u):
                if exists(t):
                    round_ = t // DEEP if isinstance(t, int) else None
                    wait_rows(pe, t, u)
                    wait(pe, x_ok, t - 1)
                    for k in range(KC):
                        mm = nc.tensor.transpose(psX[:, u % 2, k * P:(k + 1) * P], rows[:, u, k * P:(k + 1) * P],
                                                 env.ident[:])
                    mm.then_inc(x_done, 1)
                if exists(t - 1):
                    n = (u + 1) % 2
                    e = expert_of(pe, t - 1)
                    pe.wait_ge(x_ok, t)
                    wait(pe, act_ok, t - 2)
                    for k in range(KC):
                        mm = nc.tensor.matmul(psGU[:, n, 0:2 * INTER], xT[:, n, k * P:(k + 1) * P],
                                              gu_w[:, bass.ds(e, 1), k].rearrange("p o n -> p (o n)"),
                                              start=(k == 0), stop=(k == KC - 1))
                    mm.then_inc(gu_done, 1)
                if exists(t - 2):
                    pe.wait_ge(act_ok, t - 1)
                    wait(pe, a_ok, t - 3)
                    nc.tensor.transpose(psA[:, u % 2, 0:P], act_e[:, u % 2], env.ident[:]).then_inc(a_done, 1)
                if exists(t - 3):
                    n = (u + 1) % 2
                    e = expert_of(pe, t - 3)
                    pe.wait_ge(a_ok, t - 2)
                    wait(pe, y_ok, t - 4)
                    nc.tensor.matmul(psY[:, n, 0:D], actT[:, n], down_w[:, bass.ds(e, 1)].rearrange("p o n -> p (o n)"),
                                     start=True, stop=True).then_inc(y_done, 1)

            def wait_rows(eng, t, u):
                eng.wait_ge(rows_in[u], 16 * (t // DEEP + 1) if isinstance(t, int) else (t - u) * (16 // DEEP) + 16)

            pe.wait_ge(place_in, 16)
            pe.wait_ge(weights_in, 16 * WEIGHT_LOADS)
            over_steps(pe, body)

        @block.scalar
        def _(act):
            def body(t, u):
                if exists(t):
                    act.wait_ge(x_done, t + 1)
                    wait(act, gu_done, t - 1)
                    nc.scalar.activation(xT[:, u % 2], psX[:, u % 2, 0:D], ACT.Copy).then_inc(x_ok, 1)
                if exists(t - 1):
                    n = (u + 1) % 2
                    act.wait_ge(gu_done, t)
                    wait(act, act_ok, t - 2)
                    nc.scalar.activation(silu[:, n], psGU[:, n, 0:INTER], ACT.Silu).then_inc(silu_ok, 1)

            over_steps(act, body)

        @block.vector
        def _(dve):
            def body(t, u):
                if exists(t - 2):
                    dve.wait_ge(a_done, t - 1)
                    wait(dve, y_done, t - 4)
                    nc.vector.tensor_copy(actT[:, u % 2], psA[:, u % 2, 0:P]).then_inc(a_ok, 1)
                if exists(t - 1):
                    n = (u + 1) % 2
                    dve.wait_ge(silu_ok, t)
                    wait(dve, a_done, t - 3 + 1)
                    nc.vector.tensor_tensor(act_e[:, n], psGU[:, n, INTER:2 * INTER], silu[:, n],
                                            ALU.mult).then_inc(act_ok, 1)
                if exists(t):
                    e = expert_of(dve, t)
                    dve.wait_ge(x_done, t + 1)
                    wait_round(dve, scattered[u], t, u)
                    nc.vector.tensor_copy(dest[:, u:u + 1], rows[:, u, bass.ds(D + e, 1)].bitcast(I32)
                                          ).then_inc(dest_ok, 1)
                if exists(t - 3):
                    dve.wait_ge(y_done, t - 2)
                    nc.vector.tensor_copy(y[:, (u + 1) % DEEP], psY[:, (u + 1) % 2, 0:D]).then_inc(y_ok, 1)

            def wait_round(eng, sem, t, u):
                wait(eng, sem, 16 * (t // DEEP) if isinstance(t, int) else (t - u) * (16 // DEEP))

            dve.wait_ge(place_in, 16)
            over_steps(dve, body)

        @block.gpsimd
        def _(pool):
            def body(t, u):
                if exists(t - 3):
                    n = (u + 1) % DEEP
                    pool.wait_ge(dest_ok, t - 2)
                    pool.wait_ge(y_ok, t - 2)
                    pool.wait_ge(marked, t - 2)
                    nc.gpsimd.tensor_tensor(mark[:, 0:1], mark[:, 1:2], mark[:, 1:2], ALU.add).then_inc(marked, 1)
                    nc.gpsimd.indirect_dma_start(
                        env.results[:, :], bass.IndirectOffsetOnAxis(ap=dest[:, n:n + 1], axis=0), y[:, n], None
                        ).then_inc(scattered[n], 16)

            nc.gpsimd.memset(mark[:], 0.0).then_inc(marked, 1)
            pool.wait_ge(marked, 1)
            over_steps(pool, body)
            for u in range(DEEP):
                pool.wait_ge(scattered[u], 16 * ((TILES - u + DEEP - 1) // DEEP))


def combine_phase(nc, env):
    TILES_B = S // P
    BUFS = 4
    with ExitStack() as ctx:
        def sb(name, shape, dt=F32):
            return ctx.enter_context(nc.sbuf_tensor(name, shape, dt))

        six = sb("six", [P, BUFS, TOPK, D])
        acc = sb("acc", [P, BUFS, 2, D])
        summed, ch = (env.sem("co_" + n) for n in ("summed", "chain"))
        six_in, stored = ([env.sem(f"co_{n}{u}") for u in range(BUFS)] for n in ("six_in", "stored"))
        results = env.results[0:T * TOPK].rearrange("(t p j) d -> t p j d", p=P, j=TOPK)
        out = env.out.rearrange("(t p) d -> t p d", p=P)
        block = ctx.enter_context(nc.Block())

        @block.sync
        def _(sp):
            def load(t, u):
                wait(sp, summed, t - BUFS + 1)
                sp.dma_start(six[:, u], results[bass.ds(t, 1)].rearrange("o p j d -> (o p) j d")
                             ).then_inc(six_in[u], 16)

            for u in range(BUFS):
                load(u, u)
            with sp.Fori(1, T // P // BUFS) as i:
                for u in range(BUFS):
                    load(BUFS * i + u, u)

        @block.scalar
        def _(act):
            def store(t, u):
                act.wait_ge(summed, t + 1)
                act.dma_start(out[bass.ds(t, 1)].rearrange("o p d -> (o p) d"), acc[:, u, 0]).then_inc(stored[u], 16)

            with act.Fori(0, T // P // BUFS) as i:
                for u in range(BUFS):
                    store(BUFS * i + u, u)
            for u in range(BUFS):
                act.wait_ge(stored[u], 16 * (T // P // BUFS))

        @block.vector
        def _(dve):
            chain = Chain(dve, ch)

            def tile(i, u, t, b):
                if not isinstance(i, int) or i > 0:
                    dve.wait_ge(stored[u], 16 * i)
                dve.wait_ge(six_in[u], 16 * (i + 1))
                w = env.weights[:, bass.ds(t, 1)].rearrange("p o j -> p (o j)")
                for j in range(TOPK):
                    if j == 0:
                        ins = nc.vector.tensor_scalar(acc[:, u, 1], six[:, u, 0], w[:, 0:1], None, ALU.mult)
                    else:
                        ins = nc.vector.scalar_tensor_tensor(
                            out=acc[:, u, (j + 1) % 2], in0=six[:, u, j], scalar=w[:, j:j + 1], in1=acc[:, u, j % 2],
                            op0=ALU.mult, op1=ALU.add)
                    chain.link(ins)
                last = TOPK % 2
                chain.link(nc.vector.tensor_tensor(
                    acc[:, u, 1 - last], acc[:, u, last], env.modb[:, bass.ds(b, 1), 3].rearrange("p o d -> p (o d)"),
                    ALU.mult))
                nc.vector.tensor_tensor(acc[:, u, 0], acc[:, u, 1], env.x2[:, bass.ds(t, 1)].rearrange(
                    "p o d -> p (o d)"), ALU.add).then_inc(summed, 1)

            def batch(b):
                for n in range(TILES_B):
                    i = (TILES_B // BUFS) * b + n // BUFS
                    tile(i, n % BUFS, TILES_B * b + n, b)

            batch(0)
            chain.loop(1, B, (TOPK + 1) * TILES_B, batch)


def declare(nc, env, ctx):
    def sb(name, shape, dt):
        return ctx.enter_context(nc.sbuf_tensor(name, shape, dt))

    def dram(name, shape, dt):
        return nc.dram_tensor(name, shape, dt).ap()

    env.sem = lambda name: ctx.enter_context(nc.semaphore(name))
    env.ident = sb("ident", [P, P], F32)
    env.wqkv = sb("wqkv", [P, 3, KC, D], F32)
    env.bqk = sb("bqk", [P, 2, KC], F32)
    env.bv_bc = sb("bv_bc", [P, D], F32)
    env.modc = sb("modc", [P, 4, KC, B], F32)
    env.modb = sb("modb", [P, B, 4, D], F32)
    env.qk_parts = dram("qk_parts", (2, 3, B, KC, P, S), BF16)
    env.max_d = dram("maxima", (HG * KT, P // 32, 32), BF16)
    env.x2 = sb("x2", [P, T // P, D], F32)
    env.weights = sb("weights", [P, T // P, TOPK], F32)
    env.rden_d = dram("inverse_sums", (B, H, S), F32)
    env.lists = dram("lists", (LIST_ROWS, ROW), F32)
    env.table_d = dram("tile_table", (2 * P, 2), I32)
    env.results = dram("results", (RES_ROWS, D), F32)
    env.o_d = dram("o_sums", (B, NG, P, HD, S // HD), F32)
    env.v_d = dram("v_values", (B, NG, P, KT, HG * 2 * HD), F32)


def build(nc, env, ctx):
    declare(nc, env, ctx)
    setup_phase(nc, env)
    projection_phase(nc, env)
    attention_phase(nc, env)
    route_phase(nc, env)
    expert_phase(nc, env)
    combine_phase(nc, env)


def layout(given):
    import numpy as np

    D_ = given["L0_attn_x"].shape[-1]
    w_qkv = given["L0_attn_w_qkv"].reshape(H, 3, HD, D_)
    b_qkv = given["L0_attn_b_qkv"].reshape(H, 3, HD).transpose(1, 0, 2)
    arrays = {
        "x": given["L0_attn_x"].reshape(T, D),
        "cT": given["L0_c"].T,
        "wmod": given["L0_wmod"],
        "wqkvT": w_qkv.transpose(1, 3, 0, 2).reshape(3, D, D),
        "bqk_d": b_qkv[:2].reshape(2, KC, P).transpose(2, 0, 1),
        "bv_d": b_qkv[2].reshape(1, D),
        "woT": given["L0_attn_w_o"].T,
        "bo_d": given["L0_attn_b_o"].reshape(1, D),
        "gateT": given["L0_ffn_gate_weight"].T,
        "ebias_d": given["L0_ffn_e_score_correction_bias"].reshape(1, E),
        "wsgT": np.concatenate([given["L0_ffn_shared_gate_w"].T, given["L0_ffn_shared_up_w"].T], axis=1),
        "wsdT": given["L0_ffn_shared_down_w"].T,
        "guT": given["L0_ffn_experts_gate_up"].transpose(0, 2, 1),
        "downT": given["L0_ffn_experts_down"].transpose(0, 2, 1),
    }
    return {name: np.ascontiguousarray(a) for name, a in arrays.items()}


def kernel(**inputs):
    import numpy as np
    import concourse.bacc as bacc
    from concourse.bass_utils import run_bass_kernel_spmd

    nc = bacc.Bacc("TRN2", target_bir_lowering=False, num_devices=1)
    arrays = layout({name: np.asarray(a) for name, a in inputs.items()})
    aps = {name: nc.dram_tensor(f"in_{name}_dram", a.shape, mybir.dt.from_np(a.dtype), kind="ExternalInput").ap()
           for name, a in arrays.items()}
    env = Env()
    env.x, env.cT, env.wmod, env.wqkvT = aps["x"], aps["cT"], aps["wmod"], aps["wqkvT"]
    env.bqk_d, env.bv_d, env.woT, env.bo_d = aps["bqk_d"], aps["bv_d"], aps["woT"], aps["bo_d"]
    env.gateT, env.ebias_d, env.wsgT, env.wsdT = aps["gateT"], aps["ebias_d"], aps["wsgT"], aps["wsdT"]
    env.guT, env.downT = aps["guT"], aps["downT"]
    env.out = nc.dram_tensor("out_0_dram", (T, D), F32, kind="ExternalOutput").ap()
    with ExitStack() as ctx:
        build(nc, env, ctx)
    got = run_bass_kernel_spmd(nc, [{f"in_{name}_dram": a for name, a in arrays.items()}], core_ids=[0])
    return got.results[0]["out_0_dram"].reshape(B, S, D)
```

```python
from contextlib import ExitStack

import concourse.bass as bass
from concourse import mybir
from concourse.alu_op_type import AluOpType as ALU

ACT = mybir.ActivationFunctionType
F32 = mybir.dt.float32
BF16 = mybir.dt.bfloat16
I32 = mybir.dt.int32
AX = mybir.AxisListType

P = 128
B, S, D = 4, 1024, 256
H, HD = 16, 16
T = B * S
KC = D // P
CH = 512
TPC = CH // P
CPB = S // CH
LN_EPS = 1e-5
HG = 4
NG = H // HG
KT = S // P
QROWS = 6 * HD
Q_PART = (0, 0, 0, 1, 1, 2)
K_PART = (0, 1, 2, 0, 1, 0)
HI, MID, LO = range(3)
E, TOPK = 32, 6
GROUPS, TOPG = 8, 4
EPG = E // GROUPS
INTER = 128
SHARED = 256
ROUTED_SCALE = 2.5
WORD = 4
EBITS = 5
TILES = (T * TOPK - E) // P + E
CAP = T + P
LIST_ROWS = E * CAP + E * P
ROW = D + E
RES_ROWS = T * TOPK + 2 * E * P
SA, CA, GA, SB_, CB, GB = range(6)


class Env:
    pass


def wait(eng, sem, value):
    if not isinstance(value, int) or value > 0:
        eng.wait_ge(sem, value)


class Chain:

    def __init__(self, eng, sem, base=0):
        self.eng, self.sem, self.count, self.links = eng, sem, base, 0

    def link(self, instruction):
        instruction.then_inc(self.sem, 1)
        self.count = self.count + 1
        self.links += 1
        self.eng.wait_ge(self.sem, self.count)

    def loop(self, first, end, links, body):
        start = self.count
        with self.eng.Fori(first, end) as i:
            self.count, self.links = start + (i - first) * links, 0
            body(i)
            assert self.links == links, self.links
        self.count = start + (end - first) * links


def mean_and_variance(nc, chain, mean, var, diff, stats, varied):
    even, odd = stats[:, :, 1], stats[:, :, 4]
    nc.vector.tensor_tensor(mean, even, odd, ALU.add)
    nc.vector.tensor_tensor(diff, even, odd, ALU.subtract)
    chain.link(nc.vector.tensor_tensor(var, stats[:, :, 2], stats[:, :, 5], ALU.add))
    nc.vector.tensor_scalar(mean, mean, 0.5, None, ALU.mult)
    nc.vector.tensor_scalar(var, var, 1.0 / D, LN_EPS, ALU.mult, ALU.add)
    chain.link(nc.vector.tensor_tensor(diff, diff, diff, ALU.mult))
    nc.vector.scalar_tensor_tensor(out=var, in0=diff, scalar=0.25, in1=var, op0=ALU.mult,
                                   op1=ALU.add).then_inc(varied, 1)


def inverse_deviation(nc, chain, out, scratch, std, var):
    chain.link(nc.vector.reciprocal(out, std))
    chain.link(nc.vector.tensor_tensor(scratch, out, out, ALU.mult))
    chain.link(nc.vector.tensor_tensor(scratch, scratch, var, ALU.mult))
    chain.link(nc.vector.tensor_scalar(scratch, scratch, -0.5, 1.5, ALU.mult, ALU.add))
    chain.link(nc.vector.tensor_tensor(out, out, scratch, ALU.mult))


def setup_phase(nc, env):
    with ExitStack() as ctx:
        def sb(name, shape, dt):
            return ctx.enter_context(nc.sbuf_tensor(name, shape, dt))

        cT = sb("cT", [P, KC, B], F32)
        scT = sb("scT", [P, KC, B], F32)
        sc_rep = sb("sc_rep", [P, KC, B, P], F32)
        wmod_sb = sb("wmod_sb", [P, KC, 6 * D], F32)
        sign = sb("sign", [P, 2, B, D], F32)
        mag = sb("mag", [P, 2, B, D], F32)
        psC = ctx.enter_context(nc.psum_tensor("psC", [P, 4, KC, B], F32))
        psB = ctx.enter_context(nc.psum_tensor("psB", [P, 4, 512], F32))
        loads, silu, rep, chan, bcast, copied, ch, zero = (env.sem(n) for n in (
            "setup_loads", "setup_silu", "setup_rep", "setup_chan", "setup_bcast", "setup_copied", "setup_chain",
            "setup_zero"))
        n_loads = 5
        block = ctx.enter_context(nc.Block())

        @block.sync
        def _(sp):
            sp.dma_start(cT[:], env.cT.rearrange("(k p) b -> p k b", p=P)).then_inc(loads, 16)
            sp.dma_start(wmod_sb[:], env.wmod.rearrange("(k p) n -> p k n", p=P)).then_inc(loads, 16)
            sp.dma_start(env.wqkv[:], env.wqkvT.rearrange("s (k p) n -> p s k n", p=P)).then_inc(loads, 16)
            sp.dma_start(env.bqk[:], env.bqk_d).then_inc(loads, 16)
            sp.dma_start(env.bv_bc[:], env.bv_d.to_broadcast([P, D])).then_inc(loads, 16)
            sp.wait_ge(loads, 16 * n_loads)

        @block.gpsimd
        def _(pool):
            nc.gpsimd.memset(env.ident[:], 0.0).then_inc(zero, 1)
            pool.wait_ge(zero, 1)
            nc.gpsimd.affine_select(out=env.ident[:], in_=env.ident[:], compare_op=ALU.not_equal, fill=1.0, base=0,
                                    pattern=[[-1, P]], channel_multiplier=1).then_inc(zero, 1)
            pool.wait_ge(zero, 2)

        @block.scalar
        def _(act):
            act.wait_ge(loads, 16 * n_loads)
            nc.scalar.activation(scT[:], cT[:], ACT.Silu).then_inc(silu, 1)

        @block.vector
        def _(dve):
            c = Chain(dve, ch)
            dve.wait_ge(silu, 1)
            nc.vector.tensor_copy(sc_rep[:].rearrange("p k b r -> p (k b) r"),
                                  scT[:].rearrange("p k b -> p (k b)").unsqueeze(2).to_broadcast([P, KC * B, P])
                                  ).then_inc(rep, 1)
            dve.wait_ge(chan, 1)
            c.link(nc.vector.tensor_copy(env.modc[:, 0::2], psC[:, 0::2]))
            c.link(nc.vector.tensor_scalar(env.modc[:, 1::2], psC[:, 1::2], 1.0, None, ALU.add))
            for n in range(2 * B):
                b, half = n // 2, n % 2
                dve.wait_ge(bcast, n + 1)
                nc.vector.tensor_copy(env.modb[:, b, 2 * half:2 * half + 2].rearrange("p a d -> p (a d)"),
                                      psB[:, n % 4]).then_inc(copied, 1)
            dve.wait_ge(copied, 2 * B)
            for n, kind in enumerate((0, 3)):
                g = env.modb[:, :, kind]
                c.link(nc.vector.tensor_scalar(sign[:, n], g, 0.0, 2.0, ALU.is_ge, ALU.mult))
                c.link(nc.vector.tensor_scalar(mag[:, n], g, -1.0, None, ALU.mult))
                c.link(nc.vector.tensor_tensor(mag[:, n], mag[:, n], g, ALU.max))
                c.link(nc.vector.tensor_scalar(mag[:, n], mag[:, n], 0.25, None, ALU.max))
                c.link(nc.vector.tensor_scalar(sign[:, n], sign[:, n], -1.0, None, ALU.add))
                c.link(nc.vector.tensor_tensor(g, sign[:, n], mag[:, n], ALU.mult))
            c.link(nc.vector.tensor_scalar(env.modb[:, :, 2], env.modb[:, :, 2], 1.0, None, ALU.add))

        @block.tensor
        def _(pe):
            pe.wait_ge(silu, 1)
            for n, kind in enumerate((SA, CA, SB_, CB)):
                for m in range(KC):
                    for k in range(KC):
                        last = nc.tensor.matmul(psC[:, n, m], wmod_sb[:, k, kind * D + m * P:kind * D + m * P + P],
                                                scT[:, k], start=(k == 0), stop=(k == KC - 1))
            last.then_inc(chan, 1)
            pe.wait_ge(rep, 1)
            for n in range(2 * B):
                b, half = n // 2, n % 2
                if n >= 4:
                    pe.wait_ge(copied, n - 3)
                for k in range(KC):
                    mm = nc.tensor.matmul(psB[:, n % 4], sc_rep[:, k, b],
                                          wmod_sb[:, k, 2 * D + half * 512:2 * D + half * 512 + 512],
                                          start=(k == 0), stop=(k == KC - 1))
                mm.then_inc(bcast, 1)


def projection_phase(nc, env):
    NCH = B * CPB
    QKT = 2 * KC
    with ExitStack() as ctx:
        def sb(name, shape, dt):
            return ctx.enter_context(nc.sbuf_tensor(name, shape, dt))

        xin = sb("xin", [P, 2, TPC, D], F32)
        stats = sb("stats", [P, 2, TPC, 6], F32)
        mean = sb("mean", [P, 2, TPC], F32)
        diff = sb("diff", [P, 2, TPC], F32)
        std = sb("std", [P, 2, TPC], F32)
        rstd = sb("rstd", [P, 2, TPC], F32)
        var = sb("var", [P, 2, TPC], F32)
        newton = sb("newton", [P, 2, TPC], F32)
        xhat = sb("xhat", [P, 2, TPC, D], F32)
        hT = sb("hT", [P, 2, KC, CH], F32)
        full = sb("full", [P, QKT, CH], F32)
        rest = sb("rest", [P, QKT, CH], F32)
        parts = sb("parts", [P, QKT, 3, CH], BF16)
        vst = sb("vst", [P, 2, TPC, H, 2 * HD], F32)
        psT = ctx.enter_context(nc.psum_tensor("psT", [P, KC, CH], F32))
        psQK = ctx.enter_context(nc.psum_tensor("psQK", [P, QKT, CH], F32))
        psV = ctx.enter_context(nc.psum_tensor("psV", [P, 2, 2, D], F32))
        (varied, std_ok, normed, turned, modulated, qk_done, p0_ok, r_ok, p1_ok, p2_ok, v_done, v_ok, ones_ok,
         ch) = (env.sem("proj_" + n) for n in (
            "varied", "std_ok", "normed", "turned", "modulated", "qk_done", "p0_ok", "r_ok", "p1_ok",
            "p2_ok", "v_done", "v_ok", "ones_ok", "chain"))
        x_in, v_stored = ([env.sem(f"proj_{n}{u}") for u in range(CPB)] for n in ("x_in", "v_stored"))
        qk_stored = [env.sem(f"proj_qk_stored{j}") for j in range(QKT)]
        x_d = env.x.rearrange("(c i p) d -> c p i d", i=TPC, p=P)

        def over_batches(eng, body):
            body(0, False)
            with eng.Fori(1, B - 1) as b:
                body(b, False)
            body(B - 1, True)

        block = ctx.enter_context(nc.Block())

        @block.sync
        def _(sp):
            def load(c, u):
                wait(sp, normed, c - 1)
                sp.dma_start(xin[:, u], x_d[bass.ds(c, 1)].rearrange("o p i d -> (o p) i d")).then_inc(x_in[u], 16)

            def store(c, b, u):
                for j in range(QKT):
                    sp.wait_ge(p2_ok, QKT * c + j + 1)
                    sp.dma_start(env.qk_parts[j // KC, :, bass.ds(b, 1), j % KC, :, u * CH:(u + 1) * CH].rearrange(
                        "s o p t -> p (s o) t"), parts[:, j]).then_inc(qk_stored[j], 16)
                sp.wait_ge(v_ok, 2 * (c + 1))
                for g in range(NG):
                    sp.dma_start(env.v_d[bass.ds(b, 1), g, :, u * TPC:(u + 1) * TPC].rearrange("o p k n -> (o p) k n"),
                                 vst[:, u, :, g * HG:(g + 1) * HG, :].rearrange("p i h n -> p i (h n)")
                                 ).then_inc(v_stored[u], 16)

            def body(b, last):
                for u in range(CPB):
                    c = b * CPB + u
                    if not last:
                        load(c + 2, u)
                    store(c, b, u)

            load(0, 0)
            load(1, 1)
            over_batches(sp, body)
            for j in range(QKT):
                sp.wait_ge(qk_stored[j], 16 * NCH)
            for u in range(CPB):
                sp.wait_ge(v_stored[u], 16 * NG * B)

        @block.vector
        def _(dve):
            LN_LINKS = 8

            def norm(c, b, u):
                chain = Chain(dve, ch, LN_LINKS * c)
                dve.wait_ge(x_in[u], 16 * (b + 1))
                for i in range(TPC):
                    ins = nc.vector.bn_stats(stats[:, u, i], xin[:, u, i])
                chain.link(ins)
                mean_and_variance(nc, chain, mean[:, u], var[:, u], diff[:, u], stats[:, u], varied)
                dve.wait_ge(std_ok, c + 1)
                inverse_deviation(nc, chain, rstd[:, u], newton[:, u], std[:, u], var[:, u])
                wait(dve, turned, KC * (c - 1))
                for i in range(TPC):
                    ins = nc.vector.tensor_scalar(xhat[:, u, i], xin[:, u, i], mean[:, u, i:i + 1], rstd[:, u, i:i + 1],
                                                  ALU.subtract, ALU.mult)
                ins.then_inc(normed, 1)

            def split(c, j):
                dve.wait_ge(p0_ok, QKT * c + j + 1)
                nc.vector.tensor_tensor(rest[:, j], full[:, j], parts[:, j, HI], ALU.subtract).then_inc(r_ok, 1)

            def split_last(c, j):
                dve.wait_ge(p1_ok, QKT * c + j + 1)
                nc.vector.tensor_tensor(parts[:, j, LO], rest[:, j], parts[:, j, MID], ALU.subtract).then_inc(p2_ok, 1)

            def values(c, b, u):
                for n in range(2):
                    dve.wait_ge(v_done, 2 * c + n + 1)
                    if n == 0:
                        wait(dve, v_stored[u], 16 * NG * b)
                    nc.vector.tensor_tensor(
                        vst[:, u, 2 * n:2 * n + 2, :, 0:HD], psV[:, n].rearrange("p i (h d) -> p i h d", h=H),
                        env.bv_bc[:].rearrange("p (h d) -> p h d", h=H).unsqueeze(1).to_broadcast([P, 2, H, HD]),
                        ALU.add).then_inc(v_ok, 1)

            def body(b, last):
                for u in range(CPB):
                    c = b * CPB + u
                    if not (last and u == CPB - 1):
                        norm(c + 1, b + (u + 1) // 2, (u + 1) % 2)
                    for j in range(QKT):
                        split(c, j)
                        if j:
                            split_last(c, j - 1)
                    split_last(c, QKT - 1)
                    values(c, b, u)

            nc.vector.memset(vst[:, :, :, :, HD:2 * HD], 1.0).then_inc(ones_ok, 1)
            dve.wait_ge(ones_ok, 1)
            norm(0, 0, 0)
            over_batches(dve, body)

        @block.scalar
        def _(act):
            def deviation(c, u):
                act.wait_ge(varied, c + 1)
                nc.scalar.activation(std[:, u], var[:, u], ACT.Sqrt).then_inc(std_ok, 1)

            def modulate(c, b, u):
                for k in range(KC):
                    act.wait_ge(turned, KC * c + k + 1)
                    if k == 0:
                        wait(act, v_done, 2 * (c - 1))
                    nc.scalar.activation(hT[:, u, k], psT[:, k], ACT.Identity, bias=env.modc[:, 0, k, bass.ds(b, 1)],
                                         scale=env.modc[:, 1, k, bass.ds(b, 1)]).then_inc(modulated, 1)

            def evacuate(c, j):
                act.wait_ge(qk_done, QKT * c + j + 1)
                wait(act, qk_stored[j], 16 * c)
                bias = env.bqk[:, j // KC, j % KC:j % KC + 1]
                nc.scalar.activation(full[:, j], psQK[:, j], ACT.Identity, bias=bias)
                nc.scalar.activation(parts[:, j, HI], psQK[:, j], ACT.Identity, bias=bias).then_inc(p0_ok, 1)

            def second(c, j):
                act.wait_ge(r_ok, QKT * c + j + 1)
                nc.scalar.activation(parts[:, j, MID], rest[:, j], ACT.Copy).then_inc(p1_ok, 1)

            def body(b, last):
                for u in range(CPB):
                    c = b * CPB + u
                    if not (last and u == CPB - 1):
                        deviation(c + 1, (u + 1) % 2)
                    for j in range(QKT):
                        evacuate(c, j)
                        if j:
                            second(c, j - 1)
                    second(c, QKT - 1)
                    if not (last and u == CPB - 1):
                        modulate(c + 1, b + (u + 1) // 2, (u + 1) % 2)

            deviation(0, 0)
            modulate(0, 0, 0)
            over_batches(act, body)

        @block.tensor
        def _(pe):
            def turn(c, u):
                pe.wait_ge(normed, c + 1)
                wait(pe, modulated, KC * c)
                for k in range(KC):
                    for i in range(TPC):
                        mm = nc.tensor.transpose(psT[:, k, i * P:(i + 1) * P], xhat[:, u, i, k * P:(k + 1) * P],
                                                 env.ident[:])
                    mm.then_inc(turned, 1)

            def queries_keys(c, u):
                pe.wait_ge(modulated, KC * (c + 1))
                for j in range(QKT):
                    wait(pe, p0_ok, QKT * (c - 1) + j + 1)
                    for k in range(KC):
                        mm = nc.tensor.matmul(psQK[:, j], env.wqkv[:, j // KC, k, (j % KC) * P:(j % KC) * P + P],
                                              hT[:, u, k], start=(k == 0), stop=(k == KC - 1))
                    mm.then_inc(qk_done, 1)

            def values(c, u):
                for n in range(2):
                    wait(pe, v_ok, 2 * (c - 1) + n + 1)
                    for i in range(2):
                        for k in range(KC):
                            mm = nc.tensor.matmul(psV[:, n, i], hT[:, u, k, (2 * n + i) * P:(2 * n + i + 1) * P],
                                                  env.wqkv[:, 2, k, :], start=(k == 0), stop=(k == KC - 1))
                    mm.then_inc(v_done, 1)

            def body(b, last):
                for u in range(CPB):
                    c = b * CPB + u
                    queries_keys(c, u)
                    if not (last and u == CPB - 1):
                        turn(c + 1, (u + 1) % 2)
                    values(c, u)

            turn(0, 0)
            over_batches(pe, body)


def attention_phase(nc, env):
    QH = S // 512
    STEPS = QH * KT
    PIECES = HG * (S // P) * 2
    RING = 3
    AHEAD = 3
    LOADS = 13
    NGR = B * NG
    with ExitStack() as ctx:
        def sb(name, shape, dt):
            return ctx.enter_context(nc.sbuf_tensor(name, shape, dt))

        qa = [sb(f"q_rows{g}", [QROWS + 1, HG, S], BF16) for g in range(NG)]
        ka = [sb(f"k_rows{g}", [QROWS + 1, HG, S], BF16) for g in range(NG)]
        va = [sb(f"v_cols{g}", [P, KT, HG * 2 * HD], F32) for g in range(NG)]
        probs = sb("probs", [P, 2, HG, 512], F32)
        o_sb = sb("o_sb", [P, HD, S // HD], F32)
        den = sb("den", [HG * HD, S // HD], F32)
        inverse = sb("inverse", [HG * HD, S // HD], F32)
        spare_to = sb("spare_to", [P, E, E], I32)
        piece_max = sb("piece_max", [P, HG * KT, 2], F32)
        row_max = sb("row_max", [P, HG * KT], F32)
        neg_max = sb("neg_max", [P, HG * KT], BF16)
        neg_max_t = sb("neg_max_t", [P, HG * KT], BF16)
        psE = ctx.enter_context(nc.psum_tensor("psE", [P, 2, 2, 512], F32))
        psM = ctx.enter_context(nc.psum_tensor("psM", [P, RING, 512], F32))
        psO = ctx.enter_context(nc.psum_tensor("psO", [P, 512], F32))
        (ones_ok, scored, exp_ok, summed, piece_done, piece_read, max_ready, max_stored, max_there, o_read,
         o_stored, den_in, inverted, inv_stored, ch) = (
            env.sem("att_" + n) for n in ("ones_ok", "scored", "exp_ok", "summed", "piece_done", "piece_read",
                                          "max_ready", "max_stored", "max_there", "o_read", "o_stored", "den_in", "inverted", "inv_stored",
                                          "chain"))
        loaded = [env.sem(f"att_loaded{g}") for g in range(NG)]
        pads_built, spare_in, const_in = (env.sem("att_" + n) for n in ("pads_built", "spare_in", "const_in"))

        def over_batches(eng, body):
            body(0, False)
            with eng.Fori(1, B - 1) as b:
                body(b, False)
            body(B - 1, True)

        def pieces_of(n):
            return range(PIECES * n // STEPS, PIECES * (n + 1) // STEPS)

        block = ctx.enter_context(nc.Block())

        @block.sync
        def _(sp):
            def load(b, g):
                for r in range(6):
                    for n, (rows, part) in enumerate(((qa, Q_PART[r]), (ka, K_PART[r]))):
                        sp.dma_start(
                            rows[g][HD * r:HD * (r + 1)],
                            env.qk_parts[n, part, bass.ds(b, 1), g // 2, (g % 2) * HG * HD:(g % 2 + 1) * HG * HD, :]
                            .rearrange("o (h d) t -> (o d) h t", d=HD)).then_inc(loaded[g], 16)
                sp.dma_start(va[g][:], env.v_d[bass.ds(b, 1), g].rearrange("o p k n -> (o p) k n")
                             ).then_inc(loaded[g], 16)

            def put_max(group, g):
                sp.wait_ge(max_ready, group + 1)
                for n in range(P // 32):
                    sp.dma_start(env.max_d[:, n], neg_max_t[32 * n:32 * n + 32, :]).then_inc(max_stored, 16)
                sp.wait_ge(max_stored, 4 * 16 * (group + 1))
                sp.dma_start(qa[g][QROWS:QROWS + 1].rearrange("o h t -> o (h t)"),
                             env.max_d.rearrange("h n r -> (h n r)").unsqueeze(0)).then_inc(max_there, 16)

            def store(b, g):
                sp.wait_ge(o_read, QH * (b * NG + g + 1))
                for j in range(HG):
                    at = 2 * HD * j
                    sp.dma_start(env.o_d[bass.ds(b, 1), g * HG + j].rearrange("o r d a -> (o d) r a"),
                                 o_sb[at:at + HD]).then_inc(o_stored, 16)
                    sp.dma_start(env.den_d[bass.ds(b, 1), g, j], o_sb[at + HD:at + HD + 1]).then_inc(o_stored, 16)

            def load_sums(b, g):
                sp.wait_ge(o_stored, 16 * 2 * HG * (b * NG + g + 1))
                sp.dma_start(den[:], env.den_d[bass.ds(b, 1), g].rearrange("o j r a -> (o j r) a")).then_inc(den_in, 16)

            def store_inverse(b, g):
                sp.wait_ge(inverted, b * NG + g + 1)
                sp.dma_start(env.inv_d[bass.ds(b, 1), g * HG:(g + 1) * HG].rearrange("o j r d a -> (o j r) d a"),
                             inverse[:].unsqueeze(1).to_broadcast([HG * HD, HD, S // HD])).then_inc(inv_stored, 16)

            def body(b, last):
                for g in range(NG):
                    first = isinstance(b, int) and b == 0 and g == 0
                    before = (b, g - 1) if g else (b - 1, NG - 1)
                    if not first:
                        load_sums(*before)
                        store_inverse(*before)
                    if not (last and g == NG - 1):
                        put_max(b * NG + g + 1, (g + 1) % NG)
                    if not last:
                        sp.wait_ge(summed, STEPS * (b * NG + g + 1))
                        load(b + 1, g)
                    store(b, g)

            for g in range(NG):
                load(0, g)
            put_max(0, 0)
            for to, of in ((env.wo, env.woT), (env.gate_w, env.gateT), (env.wsg, env.wsgT), (env.wsd, env.wsdT)):
                sp.dma_start(to[:], of.rearrange("(k p) n -> p k n", p=P)).then_inc(const_in, 16)
            sp.dma_start(env.bo_bc[:], env.bo_d.to_broadcast([P, D])).then_inc(const_in, 16)
            sp.dma_start(env.ebias[:], env.ebias_d.to_broadcast([P, E])).then_inc(const_in, 16)
            sp.wait_ge(pads_built, 3)
            spare = env.lists[E * CAP:LIST_ROWS].rearrange("(k p) n -> p k n", p=P)
            for k in range(E):
                sp.dma_start(spare[:, k, 0:D], env.pad_row[:, 0:D]).then_inc(spare_in, 16)
            sp.dma_start(spare[:, :, D:ROW], spare_to[:].bitcast(F32)).then_inc(spare_in, 16)
            over_batches(sp, body)
            sp.wait_ge(const_in, 16 * 6)
            sp.wait_ge(spare_in, 16 * (E + 1))
            load_sums(B - 1, NG - 1)
            store_inverse(B - 1, NG - 1)
            sp.wait_ge(inv_stored, 16 * NGR)

        @block.gpsimd
        def _(pool):
            nc.gpsimd.memset(env.pad_row[:, 0:D], 0.0).then_inc(pads_built, 1)
            nc.gpsimd.iota(env.pad_row[:, D:ROW].bitcast(I32), [[P, E]], base=T * TOPK, channel_multiplier=1
                           ).then_inc(pads_built, 1)
            nc.gpsimd.iota(spare_to[:], [[P, E], [0, E]], base=T * TOPK + E * P, channel_multiplier=1
                           ).then_inc(pads_built, 1)

        @block.vector
        def _(dve):
            LINKS = 2

            def piece_maximum(group, n):
                dve.wait_ge(piece_done, PIECES * group + n + 1)
                nc.vector.tensor_reduce(piece_max[:].rearrange("p m k -> p (m k)")[:, n:n + 1], psM[:, n % RING], AX.X,
                                        ALU.max).then_inc(piece_read, 1)

            def finish(group):
                chain = Chain(dve, ch, LINKS * group)
                dve.wait_ge(piece_read, PIECES * (group + 1))
                chain.link(nc.vector.tensor_tensor(row_max[:], piece_max[:, :, 0], piece_max[:, :, 1], ALU.max))
                chain.link(nc.vector.tensor_scalar(neg_max[:], row_max[:], -1.0, None, ALU.mult))
                wait(dve, max_stored, 4 * 16 * group)
                nc.vector.transpose(neg_max_t[:], neg_max[:]).then_inc(max_ready, 1)

            def invert(group):
                dve.wait_ge(den_in, 16 * (group + 1))
                wait(dve, inv_stored, 16 * group)
                nc.vector.reciprocal(inverse[:], den[:]).then_inc(inverted, 1)

            def body(b, last):
                for g in range(NG):
                    group = b * NG + g
                    more = not (last and g == NG - 1)
                    for n in range(PIECES):
                        if more:
                            piece_maximum(group + 1, n)
                        if n == PIECES * 3 // 4 and not (isinstance(group, int) and group == 0):
                            invert(group - 1)
                    if more:
                        finish(group + 1)

            for g in range(NG):
                nc.vector.memset(ka[g][QROWS:QROWS + 1], 1.0).then_inc(ones_ok, 1)
            for n in range(PIECES):
                piece_maximum(0, n)
            finish(0)
            over_batches(dve, body)
            invert(NGR - 1)

        @block.scalar
        def _(act):
            def copy_out(b, g, qh):
                act.wait_ge(summed, STEPS * (b * NG + g) + KT * (qh + 1))
                if qh == 0:
                    wait(act, o_stored, 16 * 2 * HG * (b * NG + g))
                nc.scalar.activation(o_sb[:, :, qh * 32:(qh + 1) * 32], psO[:].rearrange("p (a r) -> p r a", r=HD),
                                     ACT.Copy).then_inc(o_read, 1)

            def body(b, last):
                for g in range(NG):
                    for s in range(STEPS):
                        step = STEPS * (b * NG + g) + s
                        for pair in range(2):
                            act.wait_ge(scored, 2 * step + pair + 1)
                            if pair == 0:
                                wait(act, summed, step - 1)
                            nc.scalar.activation(
                                probs[:, s % 2, 2 * pair:2 * pair + 2], psE[:, pair], ACT.Exp,
                                scale=HD ** -0.5).then_inc(exp_ok, 1)
                        if s == KT:
                            copy_out(b, g, 0)
                        if s == 0 and not (isinstance(b, int) and b == 0 and g == 0):
                            copy_out(b, g - 1, 1)

            over_batches(act, body)
            copy_out(B - 1, NG - 1, 1)

        @block.tensor
        def _(pe):
            def piece(group, g, n):
                used = n - RING if n >= RING else (-1, -3, -2)[n]
                wait(pe, piece_read, PIECES * group + used + 1)
                qt, h, kh = (n // 2) % KT, n // (2 * KT), n % 2
                nc.tensor.matmul(psM[:, n % RING], qa[g][0:QROWS, h, qt * P:(qt + 1) * P],
                                 ka[g][0:QROWS, h, kh * 512:(kh + 1) * 512], start=True, stop=True
                                 ).then_inc(piece_done, 1)

            def scores(step, g, s, pair):
                wait(pe, exp_ok, 2 * (step - 1) + pair + 1)
                qh, kt = s // KT, s % KT
                for i in range(2):
                    h = 2 * pair + i
                    mm = nc.tensor.matmul(psE[:, pair, i], ka[g][:, h, kt * P:(kt + 1) * P],
                                          qa[g][:, h, qh * 512:(qh + 1) * 512], start=True, stop=True)
                mm.then_inc(scored, 1)

            def weighted_values(group, g, s):
                qh, kt = s // KT, s % KT
                pe.wait_ge(exp_ok, 2 * (STEPS * group + s) + 2)
                if kt == 0:
                    wait(pe, o_read, QH * group + qh)
                for h in range(HG):
                    mm = nc.tensor.matmul(psO[32 * h:32 * h + 32], va[g][:, kt, 32 * h:32 * h + 32],
                                          probs[:, s % 2, h], start=(kt == 0), stop=(kt == KT - 1))
                mm.then_inc(summed, 1)

            def body(b, last):
                for g in range(NG):
                    group = b * NG + g
                    pe.wait_ge(max_there, 16 * (group + 1))
                    for s in range(STEPS):
                        step = STEPS * group + s
                        to = g + 1 + (s + AHEAD) // STEPS
                        share = (s + AHEAD) % STEPS
                        pieces = [] if last and to >= NG else list(pieces_of(share))
                        if pieces and share == 0:
                            pe.wait_ge(loaded[to % NG], 16 * LOADS * (b + 1 + to // NG))
                        scores(step, g, s, 0)
                        for n in pieces[:1]:
                            piece(b * NG + to, to % NG, n)
                        scores(step, g, s, 1)
                        for n in pieces[1:2]:
                            piece(b * NG + to, to % NG, n)
                        if s:
                            weighted_values(group, g, s - 1)
                        elif not (isinstance(b, int) and b == 0 and g == 0):
                            weighted_values(group - 1, (g - 1) % NG, STEPS - 1)
                        for n in pieces[2:]:
                            piece(b * NG + to, to % NG, n)

            pe.wait_ge(ones_ok, NG)
            pe.wait_ge(loaded[0], 16 * LOADS)
            for n in range(PIECES):
                piece(0, 0, n)
            pe.wait_ge(loaded[1], 16 * LOADS)
            for share in range(AHEAD):
                for n in pieces_of(share):
                    piece(1, 1, n)
            over_batches(pe, body)
            weighted_values(NGR - 1, NG - 1, STEPS - 1)


def scatter_chunk(nc, env, u):
    for i in range(TPC):
        for j in range(TOPK):
            nc.gpsimd.indirect_dma_start(
                env.lists[:, :], bass.IndirectOffsetOnAxis(ap=env.slot6[:, u, i, j:j + 1], axis=0),
                env.rows[:, u, i, :], None).then_inc(env.scattered[u], 16)


def route_phase(nc, env):
    NCH = B * CPB
    SC = SHARED // P
    with ExitStack() as ctx:
        def sb(name, shape, dt=F32):
            return ctx.enter_context(nc.sbuf_tensor(name, shape, dt))

        def ps(name, shape, dt=F32):
            return ctx.enter_context(nc.psum_tensor(name, shape, dt))

        wo, wsd, bo_bc, gate_w, ebias, wsg = env.wo, env.wsd, env.bo_bc, env.gate_w, env.ebias, env.wsg
        wo_g, wsd_g = (sb(n, [P, KC, D]) for n in ("wo_g", "wsd_g"))
        bo_g = sb("bo_g", [P, D])
        num, inv, vals, h2T = (sb(n, [P, 2, KC, CH]) for n in ("num", "inv", "vals", "h2T"))
        xin, h2 = (sb(n, [P, 2, TPC, D]) for n in ("xin2", "h2"))
        xhat = sb("xhat2", [P, TPC, D])
        stats = sb("stats2", [P, TPC, 6])
        mean, diff, var, std, rstd, newton, wsum, wrec, tok6 = (sb(n, [P, TPC]) for n in (
            "mean2", "diff2", "var2", "std2", "rstd2", "newton2", "wsum", "wrec", "tok6"))
        rows, slot6, pad_slot, pad_row = env.rows, env.slot6, env.pad_slot, env.pad_row
        sc = sb("sc", [P, 2, TPC, E])
        sfc, masked, slot, dest = (sb(n, [P, TPC, E]) for n in ("sfc", "masked", "slot", "dest"))
        gmax, gmask, top, top_f = (sb(n, [P, TPC, 8]) for n in ("gmax", "gmask", "top", "top_f"))
        top_at = sb("top_at", [P, TPC, 8], mybir.dt.uint32)
        gmatch = sb("gmatch", [P, TPC, GROUPS, TOPG])
        hot, picked = (sb(n, [P, TPC, TOPK, E]) for n in ("hot", "picked"))
        sel = sb("sel", [P, TPC, E], BF16)
        w6 = sb("w6", [P, TPC, TOPK])
        count = sb("count", [P, TPC + 1, E])
        iota_e, list_at, pad_at, need_f, need_cum, ones_e = (sb(n, [P, E]) for n in (
            "iota_e", "list_at", "pad_at", "need_f", "need_cum", "ones_e"))
        need_i = sb("need_i", [P, E], I32)
        before, ones = (sb(n, [P, P], BF16) for n in ("before", "ones"))
        mark = sb("mark", [P, 1])
        past = sb("past", [P, 2, WORD, E])
        past_n = sb("past_n", [P, 2, E])
        tile_no, tile_e, tile_w = (sb(n, [P, 2, WORD]) for n in ("tile_no", "tile_e", "tile_w"))
        shift_w = sb("shift_w", [P, WORD])
        tile_c, tile_r = (sb(n, [P, 2]) for n in ("tile_c", "tile_r"))
        table = sb("table", [P, 2, 2], I32)
        silu, act_s = (sb(n, [P, SC, CH]) for n in ("silu", "act_s"))

        psX = ps("psX", [P, TPC, D])
        psT = ps("psT2", [P, KC, CH])
        psGP = ps("psGP", [P, 3 * TPC * E])
        psGU = ps("psGU", [P, 3, CH])
        BANK = {("g", 0): 0, ("u", 0): 1, ("g", 1): 2, ("u", 1): 0}
        logits, psP = psGP[:, 0:TPC * E], psGP[:, TPC * E:]
        (varied, std_ok, vals_ok, projected, x2_ok, h2_ok, rows_ok, turned, h2T_ok, gated, sc_ok, sel_ok,
         placed, routed, gu_done, silu_ok, a_ok, y_done, y_read, wo_ok, wsd_ok, consts, ch,
         down_in, table_ok, table_out, zeroed, marked) = (env.sem("rt_" + n) for n in (
            "varied", "std_ok", "vals_ok", "projected", "x2_ok", "h2_ok", "rows_ok", "turned", "h2T_ok",
            "gated", "sc_ok", "sel_ok", "placed", "routed", "gu_done", "silu_ok", "a_ok", "y_done",
            "y_read", "wo_ok", "wsd_ok", "consts", "chain",
            "down_in", "table_ok", "table_out", "zeroed", "marked"))
        ins = [env.sem(f"rt_in{u}") for u in range(CPB)]
        scattered = env.scattered
        x_d = env.x.rearrange("(c i p) d -> c p i d", i=TPC, p=P)
        LOADS = 2 * KC + 1
        CONSTS = 7 + WORD

        def over_batches(eng, body):
            body(0, False)
            with eng.Fori(1, B - 1) as b:
                body(b, False)
            body(B - 1, True)

        def none_before(c):
            return isinstance(c, int) and c == 0

        block = ctx.enter_context(nc.Block())

        @block.sync
        def _(sp):
            def load(c, b, u):
                wait(sp, x2_ok, c - 1)
                wait(sp, vals_ok, c - 1)
                heads = slice(u * H // CPB, (u + 1) * H // CPB)
                for m in range(KC):
                    for to, of in ((num, env.o_d), (inv, env.inv_d)):
                        sp.dma_start(
                            to[:, u, m].rearrange("p (h a) -> p h a", h=H // CPB),
                            of[bass.ds(b, 1), heads].rearrange("o h (m r) d a -> m (r d) (o h) a", m=KC)[m]
                            ).then_inc(ins[u], 16)
                sp.dma_start(xin[:, u], x_d[bass.ds(c, 1)].rearrange("o p i d -> (o p) i d")).then_inc(ins[u], 16)

            def body(b, last):
                for u in range(CPB):
                    c = b * CPB + u
                    load(c, b, u)
                    part = bass.ds(c * (E // NCH), E // NCH)
                    sp.dma_start(env.down_w[:, part], env.downT[part].rearrange("e p n -> p e n")).then_inc(down_in, 16)

            over_batches(sp, body)
            sp.wait_ge(table_ok, 1)
            for n in range(2):
                sp.dma_start(env.table_d[n * P:(n + 1) * P], table[:, n]).then_inc(table_out, 16)
            sp.wait_ge(table_out, 32)
            sp.wait_ge(down_in, 16 * NCH)

        @block.gpsimd
        def _(pool):
            g = nc.gpsimd
            floats = {"allow_small_or_imprecise_dtypes": True}
            g.memset(ones[:], 1.0).then_inc(consts, 1)
            g.iota(iota_e[:], [[1, E]], base=0, channel_multiplier=0, **floats).then_inc(consts, 1)
            g.iota(list_at[:], [[CAP, E]], base=0, channel_multiplier=0, **floats).then_inc(consts, 1)
            g.iota(pad_at[:], [[CAP, E]], base=0, channel_multiplier=1, **floats).then_inc(consts, 1)
            g.iota(tok6[:], [[TOPK * P, TPC]], base=0, channel_multiplier=TOPK, **floats).then_inc(consts, 1)
            g.iota(tile_no[:], [[P, 2], [1, WORD]], base=1 - WORD, channel_multiplier=1, **floats).then_inc(consts, 1)
            for k in range(WORD):
                g.memset(shift_w[:, k:k + 1], float(1 << (EBITS * k))).then_inc(consts, 1)
            pool.wait_ge(consts, CONSTS - 1)
            g.affine_select(out=before[:], in_=ones[:], compare_op=ALU.is_gt, fill=0.0, base=0, pattern=[[1, P]],
                            channel_multiplier=-1).then_inc(consts, 1)

            def values(c, b, u):
                pool.wait_ge(ins[u], 16 * LOADS * (b + 1))
                wait(pool, projected, c - 1)
                g.tensor_tensor(vals[:, u], num[:, u], inv[:, u], ALU.mult).then_inc(vals_ok, 1)

            def body(b, last):
                for u in range(CPB):
                    c = b * CPB + u
                    if not last:
                        values(c + 2, b + 1, u)
                    pool.wait_ge(rows_ok, c + 1)
                    pool.wait_ge(routed, c + 1)
                    wait(pool, marked, c)
                    g.tensor_tensor(mark[:], pad_row[:, 0:1], pad_row[:, 0:1], ALU.add).then_inc(marked, 1)
                    if not (last and u == CPB - 1):
                        scatter_chunk(nc, env, u)

            for u in range(CPB):
                values(u, 0, u)
            over_batches(pool, body)

        @block.scalar
        def _(act):
            a = nc.scalar

            def front(c, b, u):
                act.wait_ge(varied, c + 1)
                a.activation(std[:], var[:], ACT.Sqrt).then_inc(std_ok, 1)
                for k in range(KC):
                    act.wait_ge(turned, KC * c + k + 1)
                    if k == 0:
                        wait(act, gu_done, 2 * SC * (c - 1))
                    a.activation(h2T[:, u, k], psT[:, k], ACT.Copy).then_inc(h2T_ok, 1)
                act.wait_ge(gated, c + 1)
                wait(act, routed, c - 1)
                a.activation(sc[:, u].rearrange("p i e -> p (i e)"), logits, ACT.Sigmoid).then_inc(sc_ok, 1)

            def gate_shared(c):
                for m in range(SC):
                    act.wait_ge(gu_done, 2 * (SC * c + m) + 1)
                    wait(act, a_ok, SC * (c - 1) + m + 1)
                    a.activation(silu[:, m], psGU[:, BANK["g", m]], ACT.Silu).then_inc(silu_ok, 1)

            def copy_rows(c, b, u):
                act.wait_ge(h2_ok, c + 1)
                wait(act, scattered[u], 16 * TPC * TOPK * b)
                a.activation(rows[:, u, :, 0:D], h2[:, u], ACT.Copy).then_inc(rows_ok, 1)

            def body(b, last):
                for u in range(CPB):
                    c = b * CPB + u
                    front(c, b, u)
                    gate_shared(c)
                    copy_rows(c, b, u)

            over_batches(act, body)

        @block.vector
        def _(dve):
            v = nc.vector
            chain = Chain(dve, ch)
            link = chain.link

            def bc(ap, *shape):
                return ap.to_broadcast([P, *shape])

            def scale_out(b):
                wait(dve, projected, CPB * b)
                ga = env.modb[:, bass.ds(b, 1), 0, :]
                v.tensor_tensor(wo_g[:], wo[:], bc(ga, KC, D), ALU.mult)
                v.tensor_tensor(bo_g[:].unsqueeze(1), bo_bc[:].unsqueeze(1), ga, ALU.mult).then_inc(wo_ok, 1)
                dve.wait_ge(wo_ok, b + 1)

            def scale_shared(b):
                v.tensor_tensor(wsd_g[:], wsd[:], bc(env.modb[:, bass.ds(b, 1), 3, :], KC, D),
                                ALU.mult).then_inc(wsd_ok, 1)

            def front(c, b, u):
                def tile(i):
                    return env.x2[:, bass.ds(TPC * c + i, 1)].rearrange("p o d -> p (o d)")

                dve.wait_ge(ins[u], 16 * LOADS * (b + 1))
                link(v.tensor_tensor(xin[:, u], xin[:, u], bc(bo_g[:].unsqueeze(1), TPC, D), ALU.add))
                dve.wait_ge(projected, c + 1)
                v.tensor_tensor(env.x2[:, bass.ds(TPC * c, TPC)], psX[:], xin[:, u], ALU.add).then_inc(x2_ok, 1)
                dve.wait_ge(x2_ok, c + 1)
                v.tensor_copy(mean[:, 0:1], bo_bc[:, 0:1])
                for i in range(TPC):
                    ins_ = v.bn_stats(stats[:, i], tile(i))
                link(ins_)
                mean_and_variance(nc, chain, mean[:], var[:], diff[:], stats[:], varied)
                dve.wait_ge(std_ok, c + 1)
                inverse_deviation(nc, chain, rstd[:], newton[:], std[:], var[:])
                for i in range(TPC):
                    ins_ = v.tensor_scalar(xhat[:, i], tile(i), mean[:, i:i + 1], rstd[:, i:i + 1], ALU.subtract,
                                           ALU.mult)
                link(ins_)
                link(v.tensor_tensor(xhat[:], xhat[:], bc(env.modb[:, bass.ds(b, 1), 2, :], TPC, D), ALU.mult))
                wait(dve, turned, KC * (c - 1))
                wait(dve, rows_ok, c - 1)
                v.tensor_tensor(h2[:, u], xhat[:], bc(env.modb[:, bass.ds(b, 1), 1, :], TPC, D),
                                ALU.add).then_inc(h2_ok, 1)
                dve.wait_ge(h2_ok, c + 1)

            def best(of):
                v.tensor_copy(top_f[:, :, 0:1], of[:, :, 0:1])
                for i in range(TPC):
                    ins_ = v.max(top[:, i], of[:, i])
                link(ins_)
                v.tensor_copy(top_f[:, :, 0:1], of[:, :, 0:1])
                for i in range(TPC):
                    ins_ = v.max_index(top_at[:, i], top[:, i], of[:, i])
                link(ins_)
                link(v.tensor_copy(top_f[:], top_at[:]))

            def pick(of, out):
                link(v.tensor_tensor(picked[:], hot[:], bc(of.unsqueeze(2), TPC, TOPK, E), ALU.mult))
                with nc.allow_low_precision(reason="whole numbers below 2 ** 24, or float32"):
                    link(v.tensor_reduce(out, picked[:], AX.X, ALU.add))

            def route(c, b, u):
                dve.wait_ge(sc_ok, c + 1)
                link(v.tensor_tensor(sfc[:], sc[:, u], bc(ebias[:].unsqueeze(1), TPC, E), ALU.add))
                link(v.tensor_reduce(gmax[:], sfc[:].rearrange("p i (g k) -> p i g k", g=GROUPS), AX.X, ALU.max))
                best(gmax)
                link(v.tensor_tensor(gmatch[:], bc(iota_e[:, 0:GROUPS].unsqueeze(1).unsqueeze(3), TPC, GROUPS, TOPG),
                                     bc(top_f[:, :, 0:TOPG].unsqueeze(2), TPC, GROUPS, TOPG), ALU.is_equal))
                link(v.tensor_reduce(gmask[:], gmatch[:], AX.X, ALU.max))
                for i in range(TPC):
                    ins_ = v.tensor_tensor(masked[:, i].rearrange("p (g k) -> p g k", g=GROUPS),
                                           sfc[:, i].rearrange("p (g k) -> p g k", g=GROUPS),
                                           bc(gmask[:, i].unsqueeze(2), GROUPS, EPG), ALU.mult)
                link(ins_)
                best(masked)
                link(v.tensor_tensor(hot[:], bc(iota_e[:].unsqueeze(1).unsqueeze(1), TPC, TOPK, E),
                                     bc(top_f[:, :, 0:TOPK].unsqueeze(3), TPC, TOPK, E), ALU.is_equal))
                with nc.allow_low_precision(reason="zeros and ones"):
                    v.tensor_reduce(sel[:], hot[:].rearrange("p i j e -> p i e j"), AX.X, ALU.max).then_inc(sel_ok, 1)
                pick(sc[:, u], w6[:])
                link(v.tensor_reduce(wsum[:], w6[:], AX.X, ALU.add))
                link(v.tensor_scalar(wsum[:], wsum[:], 1e-20, None, ALU.add))
                link(v.reciprocal(wrec[:], wsum[:]))
                v.scalar_tensor_tensor(out=env.weights[:, bass.ds(TPC * c, TPC)], in0=w6[:], scalar=ROUTED_SCALE,
                                       in1=bc(wrec[:].unsqueeze(2), TPC, TOPK), op0=ALU.mult, op1=ALU.mult)
                dve.wait_ge(placed, c + 1)
                for i in range(TPC):
                    link(v.tensor_tensor(count[:, i + 1], psP[:, (TPC + i) * E:(TPC + i + 1) * E], count[:, i],
                                         ALU.add))
                link(v.tensor_tensor(slot[:], psP[:, 0:TPC * E].rearrange("p (i e) -> p i e", i=TPC),
                                     count[:, 0:TPC], ALU.add))
                link(v.tensor_tensor(slot[:], slot[:], bc(list_at[:].unsqueeze(1), TPC, E), ALU.add))
                wait(dve, scattered[u], 16 * TPC * TOPK * b)
                pick(slot[:], slot6[:, u])
                link(v.tensor_tensor(picked[:], hot[:], bc(iota_e[:, 0:TOPK].unsqueeze(1).unsqueeze(3), TPC, TOPK, E),
                                     ALU.mult))
                link(v.tensor_reduce(dest[:], picked[:].rearrange("p i j e -> p i e j"), AX.X, ALU.max))
                v.tensor_tensor(rows[:, u, :, D:ROW].bitcast(I32), dest[:], bc(tok6[:].unsqueeze(2), TPC, E),
                                ALU.add).then_inc(routed, 1)
                dve.wait_ge(routed, c + 1)
                v.tensor_copy(count[:, 0], count[:, TPC])
                link(v.tensor_scalar(tok6[:], tok6[:], float(TOPK * CH), None, ALU.add))

            def multiply_shared(c):
                for m in range(SC):
                    dve.wait_ge(silu_ok, SC * c + m + 1)
                    dve.wait_ge(gu_done, 2 * (SC * c + m) + 2)
                    if m == 0:
                        wait(dve, y_done, c)
                    v.tensor_tensor(act_s[:, m], psGU[:, BANK["u", m]], silu[:, m], ALU.mult).then_inc(a_ok, 1)

            def add_shared(c):
                dve.wait_ge(y_done, c + 1)
                x2 = env.x2[:, bass.ds(TPC * c, TPC)]
                v.tensor_tensor(x2, psX[:], x2, ALU.add).then_inc(y_read, 1)

            v.memset(ones_e[:], 1.0).then_inc(zeroed, 1)
            v.memset(count[:, 0], 0.0).then_inc(zeroed, 1)
            dve.wait_ge(zeroed, 2)
            dve.wait_ge(consts, CONSTS)

            def body(b, last):
                for u in range(CPB):
                    c = b * CPB + u
                    if u == 0:
                        scale_out(b)
                    front(c, b, u)
                    if not none_before(c):
                        add_shared(c - 1)
                        route(c - 1, b - 1 + u, (u + 1) % 2)
                    if u == 0:
                        scale_shared(b)
                    multiply_shared(c)

            body(0, False)
            chain.loop(1, B - 1, 78, lambda b: body(b, False))
            body(B - 1, True)
            add_shared(NCH - 1)
            route(NCH - 1, B - 1, CPB - 1)
            total = count[:, TPC]
            v.tensor_tensor(pad_slot[:], total, pad_at[:], ALU.add)
            link(v.tensor_scalar(need_i[:], total, float(P - 1), None, ALU.add))
            link(v.tensor_scalar(need_i[:], need_i[:], P.bit_length() - 1, None, ALU.arith_shift_right))
            link(v.tensor_copy(need_f[:], need_i[:]))
            link(v.tensor_tensor_scan(need_cum[:], ones_e[:], need_f[:], 0.0, ALU.mult, ALU.add))
            link(v.tensor_tensor(past[:], bc(need_cum[:].unsqueeze(1).unsqueeze(1), 2, WORD, E),
                                 bc(tile_no[:].unsqueeze(3), 2, WORD, E), ALU.is_le))
            v.tensor_reduce(tile_e[:], past[:], AX.X, ALU.add)
            link(v.tensor_tensor(past_n[:], past[:, :, WORD - 1], bc(need_f[:].unsqueeze(1), 2, E), ALU.mult))
            link(v.tensor_reduce(tile_c[:], past_n[:], AX.X, ALU.add))
            link(v.tensor_tensor(tile_r[:], tile_no[:, :, WORD - 1], tile_c[:], ALU.subtract))
            v.tensor_scalar(tile_w[:], tile_e[:], float(E - 1), None, ALU.min)
            link(v.tensor_scalar(tile_c[:], tile_e[:, :, WORD - 1], float(CAP), None, ALU.mult))
            v.scalar_tensor_tensor(out=table[:, :, 0], in0=tile_r[:], scalar=float(P), in1=tile_c[:], op0=ALU.mult,
                                   op1=ALU.add)
            link(v.tensor_tensor(tile_w[:], tile_w[:], bc(shift_w[:].unsqueeze(1), 2, WORD), ALU.mult))
            with nc.allow_low_precision(reason="whole numbers below 2 ** 20"):
                v.tensor_reduce(table[:, :, 1], tile_w[:], AX.X, ALU.add).then_inc(table_ok, 1)

        @block.tensor
        def _(pe):
            t_ = nc.tensor

            def project(c, b, u):
                pe.wait_ge(vals_ok, c + 1)
                pe.wait_ge(wo_ok, b + 1)
                wait(pe, y_read, c - 1)
                for i in range(TPC):
                    for m in range(KC):
                        mm = t_.matmul(psX[:, i], vals[:, u, m, i * P:(i + 1) * P], wo_g[:, m], start=(m == 0),
                                       stop=(m == KC - 1))
                mm.then_inc(projected, 1)

            def turn(c, u):
                pe.wait_ge(h2_ok, c + 1)
                wait(pe, h2T_ok, KC * c)
                for k in range(KC):
                    for i in range(TPC):
                        mm = t_.transpose(psT[:, k, i * P:(i + 1) * P], h2[:, u, i, k * P:(k + 1) * P], env.ident[:])
                    mm.then_inc(turned, 1)

            def gate(c, u):
                pe.wait_ge(h2T_ok, KC * (c + 1))
                wait(pe, sc_ok, c)
                for i in range(TPC):
                    for k in range(KC):
                        mm = t_.matmul(logits[:, i * E:(i + 1) * E], h2T[:, u, k, i * P:(i + 1) * P], gate_w[:, k],
                                       start=(k == 0), stop=(k == KC - 1))
                mm.then_inc(gated, 1)

            def shared_in(c, u):
                for m in range(SC):
                    for n, what in enumerate(("g", "u")):
                        if m == 0 or what == "u":
                            wait(pe, a_ok, SC * c)
                        if m == 1 and what == "u":
                            pe.wait_ge(silu_ok, SC * c + 1)
                        for k in range(KC):
                            mm = t_.matmul(psGU[:, BANK[what, m]],
                                           wsg[:, k, n * SHARED + m * P:n * SHARED + (m + 1) * P], h2T[:, u, k],
                                           start=(k == 0), stop=(k == KC - 1))
                        mm.then_inc(gu_done, 1)

            def shared_out(c, b):
                pe.wait_ge(wsd_ok, b + 1)
                pe.wait_ge(a_ok, SC * (c + 1))
                if isinstance(c, int) and c == NCH - 1:
                    pe.wait_ge(x2_ok, NCH)
                else:
                    pe.wait_ge(x2_ok, c + 2)
                for i in range(TPC):
                    for m in range(SC):
                        mm = t_.matmul(psX[:, i], act_s[:, m, i * P:(i + 1) * P], wsd_g[:, m], start=(m == 0),
                                       stop=(m == SC - 1))
                mm.then_inc(y_done, 1)

            def place(c):
                pe.wait_ge(sel_ok, c + 1)
                wait(pe, routed, c)
                flat = sel[:].rearrange("p i e -> p (i e)")
                t_.matmul(psP[:, 0:TPC * E], before[:], flat, start=True, stop=True)
                t_.matmul(psP[:, TPC * E:2 * TPC * E], ones[:], flat, start=True, stop=True).then_inc(placed, 1)

            def body(b, last):
                for u in range(CPB):
                    c = b * CPB + u
                    project(c, b, u)
                    if not none_before(c):
                        shared_out(c - 1, b - 1 + u)
                    turn(c, u)
                    gate(c, u)
                    shared_in(c, u)
                    if not none_before(c):
                        place(c - 1)

            over_batches(pe, body)
            shared_out(NCH - 1, B - 1)
            place(NCH - 1)


def expert_phase(nc, env):
    DEEP = 8
    STEPS = TILES + 3
    with ExitStack() as ctx:
        def sb(name, shape, dt=F32):
            return ctx.enter_context(nc.sbuf_tensor(name, shape, dt))

        gu_w = sb("gu_w", [P, E, KC, 2 * INTER])
        place = sb("place", [1, 2 * P, 2], I32)
        rows = sb("ex_rows", [P, DEEP, ROW])
        xT = sb("ex_xT", [P, 2, D])
        silu, act_e, actT = (sb(n, [P, 2, INTER]) for n in ("ex_silu", "ex_act", "ex_actT"))
        y = sb("ex_y", [P, DEEP, D])
        dest = sb("ex_dest", [P, DEEP], I32)
        mark = sb("ex_mark", [P, 2])
        psX, psGU, psA, psY = (ctx.enter_context(nc.psum_tensor(n, [P, 2, 512], F32)) for n in (
            "ex_psX", "ex_psGU", "ex_psA", "ex_psY"))
        (weights_in, place_in, x_done, x_ok, dest_ok, gu_done, silu_ok, act_ok, a_done, a_ok, y_done, y_ok,
         marked, pads_out) = (env.sem("ex_" + n) for n in (
            "weights_in", "place_in", "x_done", "x_ok", "dest_ok", "gu_done", "silu_ok", "act_ok", "a_done", "a_ok",
            "y_done", "y_ok", "marked", "pads_out"))
        rows_in, scattered = ([env.sem(f"ex_{n}{u}") for u in range(DEEP)] for n in ("rows_in", "scattered"))
        GROUP = 4
        WEIGHT_LOADS = E // GROUP

        def over_steps(eng, body):
            for s in range(DEEP):
                body(s, s)
            with eng.Fori(1, TILES // DEEP) as i:
                for u in range(DEEP):
                    body(DEEP * i + u, u)
            for s in range(TILES // DEEP * DEEP, STEPS):
                body(s, s % DEEP)

        def exists(t):
            return not isinstance(t, int) or 0 <= t < TILES

        def experts(eng):
            words = {}

            def expert(t, u, back):
                k, n = divmod(u - back + WORD - 1, WORD)
                if isinstance(t, int):
                    key = (t - u) // DEEP, k
                else:
                    key = "round", k
                if key not in words:
                    words[key] = eng.value_load(place[0:1, bass.ds(t - u + WORD * k, 1), 1], min_val=0,
                                                max_val=(1 << EBITS * WORD) - 1)
                return (words[key] >> (EBITS * n)) & (E - 1)

            return expert

        block = ctx.enter_context(nc.Block())

        @block.sync
        def _(sp):
            sp.dma_start(place[:], env.table_d.unsqueeze(0)).then_inc(place_in, 16)
            for e in range(0, E, GROUP):
                sp.dma_start(gu_w[:, e:e + GROUP], env.guT[e:e + GROUP].rearrange("e (k p) n -> p e k n", p=P)
                             ).then_inc(weights_in, 16)
            sp.wait_ge(place_in, 16)
            sp.wait_ge(marked, 1)

            def body(t, u):
                if exists(t):
                    row = sp.value_load(place[0:1, bass.ds(t, 1), 0], min_val=0, max_val=LIST_ROWS - P)
                    wait(sp, x_done, t - DEEP + 1)
                    wait(sp, dest_ok, t - DEEP + 1)
                    sp.dma_start(rows[:, u], env.lists[bass.ds(row, P)]).then_inc(rows_in[u], 16)

            over_steps(sp, body)

        @block.tensor
        def _(pe):
            expert = experts(pe)

            def body(t, u):
                if exists(t):
                    wait_rows(pe, t, u)
                    wait(pe, x_ok, t - 1)
                    for k in range(KC):
                        mm = nc.tensor.transpose(psX[:, u % 2, k * P:(k + 1) * P], rows[:, u, k * P:(k + 1) * P],
                                                 env.ident[:])
                    mm.then_inc(x_done, 1)
                if exists(t - 1):
                    n = (u + 1) % 2
                    e = expert(t, u, 1)
                    pe.wait_ge(x_ok, t)
                    wait(pe, act_ok, t - 2)
                    for k in range(KC):
                        mm = nc.tensor.matmul(psGU[:, n, 0:2 * INTER], xT[:, n, k * P:(k + 1) * P],
                                              gu_w[:, bass.ds(e, 1), k].rearrange("p o n -> p (o n)"),
                                              start=(k == 0), stop=(k == KC - 1))
                    mm.then_inc(gu_done, 1)
                if exists(t - 2):
                    pe.wait_ge(act_ok, t - 1)
                    wait(pe, a_ok, t - 3)
                    nc.tensor.transpose(psA[:, u % 2, 0:P], act_e[:, u % 2], env.ident[:]).then_inc(a_done, 1)
                if exists(t - 3):
                    n = (u + 1) % 2
                    e = expert(t, u, 3)
                    pe.wait_ge(a_ok, t - 2)
                    wait(pe, y_ok, t - 4)
                    nc.tensor.matmul(psY[:, n, 0:D], actT[:, n], env.down_w[:, bass.ds(e, 1)].rearrange("p o n -> p (o n)"),
                                     start=True, stop=True).then_inc(y_done, 1)

            def wait_rows(eng, t, u):
                eng.wait_ge(rows_in[u], 16 * (t // DEEP + 1) if isinstance(t, int) else (t - u) * (16 // DEEP) + 16)

            pe.wait_ge(place_in, 16)
            pe.wait_ge(weights_in, 16 * WEIGHT_LOADS)
            over_steps(pe, body)

        @block.scalar
        def _(act):
            def body(t, u):
                if exists(t):
                    act.wait_ge(x_done, t + 1)
                    wait(act, gu_done, t - 1)
                    nc.scalar.activation(xT[:, u % 2], psX[:, u % 2, 0:D], ACT.Copy).then_inc(x_ok, 1)
                if exists(t - 1):
                    n = (u + 1) % 2
                    act.wait_ge(gu_done, t)
                    wait(act, act_ok, t - 2)
                    nc.scalar.activation(silu[:, n], psGU[:, n, 0:INTER], ACT.Silu).then_inc(silu_ok, 1)

            with act.Fori(0, E) as e:
                end = act.value_load(env.pad_slot[0:1, bass.ds(e, 1)], min_val=0, max_val=LIST_ROWS - P)
                act.dma_start(env.lists[bass.ds(end, P)], env.pad_row[:]).then_inc(pads_out, 16)
            over_steps(act, body)

        @block.vector
        def _(dve):
            expert = experts(dve)

            def body(t, u):
                if exists(t - 2):
                    dve.wait_ge(a_done, t - 1)
                    wait(dve, y_done, t - 4)
                    nc.vector.tensor_copy(actT[:, u % 2], psA[:, u % 2, 0:P]).then_inc(a_ok, 1)
                if exists(t - 1):
                    n = (u + 1) % 2
                    dve.wait_ge(silu_ok, t)
                    wait(dve, a_done, t - 3 + 1)
                    nc.vector.tensor_tensor(act_e[:, n], psGU[:, n, INTER:2 * INTER], silu[:, n],
                                            ALU.mult).then_inc(act_ok, 1)
                if exists(t):
                    e = expert(t, u, 0)
                    dve.wait_ge(x_done, t + 1)
                    wait_round(dve, scattered[u], t, u)
                    nc.vector.tensor_copy(dest[:, u:u + 1], rows[:, u, bass.ds(D + e, 1)].bitcast(I32)
                                          ).then_inc(dest_ok, 1)
                if exists(t - 3):
                    dve.wait_ge(y_done, t - 2)
                    nc.vector.tensor_copy(y[:, (u - 3) % DEEP], psY[:, (u + 1) % 2, 0:D]).then_inc(y_ok, 1)

            def wait_round(eng, sem, t, u):
                wait(eng, sem, 16 * (t // DEEP) if isinstance(t, int) else (t - u) * (16 // DEEP))

            dve.wait_ge(place_in, 16)
            over_steps(dve, body)

        @block.gpsimd
        def _(pool):
            def body(t, u):
                if exists(t - 3):
                    n = (u - 3) % DEEP
                    pool.wait_ge(dest_ok, t - 2)
                    pool.wait_ge(y_ok, t - 2)
                    pool.wait_ge(marked, t - 2)
                    nc.gpsimd.tensor_tensor(mark[:, 0:1], mark[:, 1:2], mark[:, 1:2], ALU.add).then_inc(marked, 1)
                    nc.gpsimd.indirect_dma_start(
                        env.results[:, :], bass.IndirectOffsetOnAxis(ap=dest[:, n:n + 1], axis=0), y[:, n], None
                        ).then_inc(scattered[n], 16)

            scatter_chunk(nc, env, CPB - 1)
            for u in range(CPB):
                pool.wait_ge(env.scattered[u], 16 * B * TPC * TOPK)
            pool.wait_ge(pads_out, 16 * E)
            nc.gpsimd.memset(mark[:], 0.0).then_inc(marked, 1)
            pool.wait_ge(marked, 1)
            over_steps(pool, body)
            for u in range(DEEP):
                pool.wait_ge(scattered[u], 16 * ((TILES - u + DEEP - 1) // DEEP))


def combine_phase(nc, env):
    TILES_B = S // P
    BUFS = 4
    with ExitStack() as ctx:
        def sb(name, shape, dt=F32):
            return ctx.enter_context(nc.sbuf_tensor(name, shape, dt))

        six = sb("six", [P, BUFS, TOPK, D])
        acc = sb("acc", [P, BUFS, 2, D])
        summed, ch = (env.sem("co_" + n) for n in ("summed", "chain"))
        six_in, stored = ([env.sem(f"co_{n}{u}") for u in range(BUFS)] for n in ("six_in", "stored"))
        results = env.results[0:T * TOPK].rearrange("(t p j) d -> t p j d", p=P, j=TOPK)
        out = env.out.rearrange("(t p) d -> t p d", p=P)
        block = ctx.enter_context(nc.Block())

        @block.sync
        def _(sp):
            def load(t, u):
                wait(sp, summed, t - BUFS + 1)
                sp.dma_start(six[:, u], results[bass.ds(t, 1)].rearrange("o p j d -> (o p) j d")
                             ).then_inc(six_in[u], 16)

            for u in range(BUFS):
                load(u, u)
            with sp.Fori(1, T // P // BUFS) as i:
                for u in range(BUFS):
                    load(BUFS * i + u, u)

        @block.scalar
        def _(act):
            def store(t, u):
                act.wait_ge(summed, t + 1)
                act.dma_start(out[bass.ds(t, 1)].rearrange("o p d -> (o p) d"), acc[:, u, 0]).then_inc(stored[u], 16)

            with act.Fori(0, T // P // BUFS) as i:
                for u in range(BUFS):
                    store(BUFS * i + u, u)
            for u in range(BUFS):
                act.wait_ge(stored[u], 16 * (T // P // BUFS))

        @block.vector
        def _(dve):
            chain = Chain(dve, ch)

            def tile(i, u, t, b):
                if not isinstance(i, int) or i > 0:
                    dve.wait_ge(stored[u], 16 * i)
                dve.wait_ge(six_in[u], 16 * (i + 1))
                w = env.weights[:, bass.ds(t, 1)].rearrange("p o j -> p (o j)")
                for j in range(TOPK):
                    if j == 0:
                        ins = nc.vector.tensor_scalar(acc[:, u, 1], six[:, u, 0], w[:, 0:1], None, ALU.mult)
                    else:
                        ins = nc.vector.scalar_tensor_tensor(
                            out=acc[:, u, (j + 1) % 2], in0=six[:, u, j], scalar=w[:, j:j + 1], in1=acc[:, u, j % 2],
                            op0=ALU.mult, op1=ALU.add)
                    chain.link(ins)
                last = TOPK % 2
                chain.link(nc.vector.tensor_tensor(
                    acc[:, u, 1 - last], acc[:, u, last], env.modb[:, bass.ds(b, 1), 3].rearrange("p o d -> p (o d)"),
                    ALU.mult))
                nc.vector.tensor_tensor(acc[:, u, 0], acc[:, u, 1], env.x2[:, bass.ds(t, 1)].rearrange(
                    "p o d -> p (o d)"), ALU.add).then_inc(summed, 1)

            def batch(b):
                for n in range(TILES_B):
                    i = (TILES_B // BUFS) * b + n // BUFS
                    tile(i, n % BUFS, TILES_B * b + n, b)

            batch(0)
            chain.loop(1, B, (TOPK + 1) * TILES_B, batch)


def declare(nc, env, ctx):
    def sb(name, shape, dt):
        return ctx.enter_context(nc.sbuf_tensor(name, shape, dt))

    def dram(name, shape, dt):
        return nc.dram_tensor(name, shape, dt).ap()

    env.sem = lambda name: ctx.enter_context(nc.semaphore(name))
    env.ident = sb("ident", [P, P], F32)
    env.modc = sb("modc", [P, 4, KC, B], F32)
    env.modb = sb("modb", [P, B, 4, D], F32)
    env.qk_parts = dram("qk_parts", (2, 3, B, KC, P, S), BF16)
    env.v_d = dram("v_values", (B, NG, P, KT, HG * 2 * HD), F32)
    env.max_d = dram("maxima", (HG * KT, P // 32, 32), BF16)
    env.o_d = dram("o_sums", (B, H, HD, HD, S // HD), F32)
    env.inv_d = dram("inverse_sums", (B, H, HD, HD, S // HD), F32)
    env.den_d = dram("sums", (B, NG, HG, HD, S // HD), F32)
    env.lists = dram("lists", (LIST_ROWS, ROW), F32)
    env.table_d = dram("tile_table", (2 * P, 2), I32)
    env.results = dram("results", (RES_ROWS, D), F32)


def declare_projection(nc, env, ctx):
    env.wqkv = ctx.enter_context(nc.sbuf_tensor("wqkv", [P, 3, KC, D], F32))
    env.bqk = ctx.enter_context(nc.sbuf_tensor("bqk", [P, 2, KC], F32))
    env.bv_bc = ctx.enter_context(nc.sbuf_tensor("bv_bc", [P, D], F32))


def declare_routing(nc, env, ctx):
    for_sb = {"wo": [P, KC, D], "wsd": [P, KC, D], "bo_bc": [P, D], "gate_w": [P, KC, E], "ebias": [P, E],
              "wsg": [P, KC, 2 * SHARED], "pad_row": [P, ROW]}
    env.wo, env.wsd, env.bo_bc, env.gate_w, env.ebias, env.wsg, env.pad_row = (
        ctx.enter_context(nc.sbuf_tensor(name, shape, F32)) for name, shape in for_sb.items())


def declare_experts(nc, env, ctx):
    env.x2 = ctx.enter_context(nc.sbuf_tensor("x2", [P, T // P, D], F32))
    env.weights = ctx.enter_context(nc.sbuf_tensor("weights", [P, T // P, TOPK], F32))
    env.rows = ctx.enter_context(nc.sbuf_tensor("rows", [P, 2, TPC, ROW], F32))
    env.slot6 = ctx.enter_context(nc.sbuf_tensor("slot6", [P, 2, TPC, TOPK], I32))
    env.pad_slot = ctx.enter_context(nc.sbuf_tensor("pad_slot", [P, E], I32))
    env.scattered = [env.sem(f"scattered{u}") for u in range(CPB)]
    env.down_w = ctx.enter_context(nc.sbuf_tensor("down_w", [P, E, D], F32))


def build(nc, env, ctx):
    declare(nc, env, ctx)
    with ExitStack() as projection_ctx:
        declare_projection(nc, env, projection_ctx)
        setup_phase(nc, env)
        projection_phase(nc, env)
    declare_routing(nc, env, ctx)
    attention_phase(nc, env)
    declare_experts(nc, env, ctx)
    route_phase(nc, env)
    expert_phase(nc, env)
    combine_phase(nc, env)


def layout(given):
    import numpy as np

    D_ = given["L0_attn_x"].shape[-1]
    w_qkv = given["L0_attn_w_qkv"].reshape(H, 3, HD, D_)
    b_qkv = given["L0_attn_b_qkv"].reshape(H, 3, HD).transpose(1, 0, 2)
    arrays = {
        "x": given["L0_attn_x"].reshape(T, D),
        "cT": given["L0_c"].T,
        "wmod": given["L0_wmod"],
        "wqkvT": w_qkv.transpose(1, 3, 0, 2).reshape(3, D, D),
        "bqk_d": b_qkv[:2].reshape(2, KC, P).transpose(2, 0, 1),
        "bv_d": b_qkv[2].reshape(1, D),
        "woT": given["L0_attn_w_o"].T,
        "bo_d": given["L0_attn_b_o"].reshape(1, D),
        "gateT": given["L0_ffn_gate_weight"].T,
        "ebias_d": given["L0_ffn_e_score_correction_bias"].reshape(1, E),
        "wsgT": np.concatenate([given["L0_ffn_shared_gate_w"].T, given["L0_ffn_shared_up_w"].T], axis=1),
        "wsdT": given["L0_ffn_shared_down_w"].T,
        "guT": given["L0_ffn_experts_gate_up"].transpose(0, 2, 1),
        "downT": given["L0_ffn_experts_down"].transpose(0, 2, 1),
    }
    return {name: np.ascontiguousarray(a) for name, a in arrays.items()}


def kernel(**inputs):
    import numpy as np
    import concourse.bacc as bacc
    from concourse.bass_utils import run_bass_kernel_spmd

    nc = bacc.Bacc("TRN2", target_bir_lowering=False, num_devices=1)
    arrays = layout({name: np.asarray(a) for name, a in inputs.items()})
    aps = {name: nc.dram_tensor(f"in_{name}_dram", a.shape, mybir.dt.from_np(a.dtype), kind="ExternalInput").ap()
           for name, a in arrays.items()}
    env = Env()
    env.x, env.cT, env.wmod, env.wqkvT = aps["x"], aps["cT"], aps["wmod"], aps["wqkvT"]
    env.bqk_d, env.bv_d, env.woT, env.bo_d = aps["bqk_d"], aps["bv_d"], aps["woT"], aps["bo_d"]
    env.gateT, env.ebias_d, env.wsgT, env.wsdT = aps["gateT"], aps["ebias_d"], aps["wsgT"], aps["wsdT"]
    env.guT, env.downT = aps["guT"], aps["downT"]
    env.out = nc.dram_tensor("out_0_dram", (T, D), F32, kind="ExternalOutput").ap()
    with ExitStack() as ctx:
        build(nc, env, ctx)
    got = run_bass_kernel_spmd(nc, [{f"in_{name}_dram": a for name, a in arrays.items()}], core_ids=[0])
    return got.results[0]["out_0_dram"].reshape(B, S, D)
```
